# Optimizing a Trainium2 kernel written in Bass

```python
import numpy as np
import jax
import jax.numpy as jnp

def _softmax(x, axis=-1):
    return jax.nn.softmax(x, axis=axis)

def _gelu(x):
    return jax.nn.gelu(x, approximate=True)

def _silu(x):
    return jax.nn.silu(x)

def _sigmoid(x):
    return jax.nn.sigmoid(x)

def _layernorm(x, axis=-1, eps=1e-05):
    m = jnp.mean(x, axis=axis, keepdims=True)
    v = jnp.var(x, axis=axis, keepdims=True)
    return (x - m) / jnp.sqrt(v + eps)

def _scatter_add(tgt, idx, src, axis=0):
    return tgt.at[idx].add(src)

def _segment_sum(src, seg, n):
    return jax.ops.segment_sum(src, seg, n)
kernel_name = 'mk_xattn_ffn_d1_seqx_r4_51f25f'

def setup_inputs(seed: int=0):
    np.random.seed(seed)
    _w = jnp.asarray

    def _rec_inputs():
        import jax
        import jax.numpy as jnp
        _rk = jax.random.key(seed)
        x = -0.000125 + 0.9999 * jax.random.normal(jax.random.fold_in(_rk, 1), (4, 512, 512), jnp.float32)
        _lenS = 512 - jax.random.randint(jax.random.fold_in(_rk, 7), (4,), 0, max(1, 512 // 4) + 1, jnp.int32)
        _lenS2 = 512 - jax.random.randint(jax.random.fold_in(_rk, 8), (4,), 0, max(1, 512 // 4) + 1, jnp.int32)
        itok_BxS_13_99985 = jax.random.randint(jax.random.fold_in(_rk, 11), (4, 512), 13, 99986, jnp.int32)
        _ctx_2048P = jax.random.normal(jax.random.fold_in(_rk, 12), (4, 16, 512), jnp.float32)
        _ctx_2048c = jax.random.dirichlet(jax.random.fold_in(_rk, 512), 0.3 * jnp.ones((16,), jnp.float32), (4, 512))
        _ctx_2048t = jnp.einsum('bsk,bkd->bsd', _ctx_2048c, _ctx_2048P)
        _ctx_2048t = _ctx_2048t * jax.lax.rsqrt(jnp.mean(jnp.square(_ctx_2048t)) + 1e-12) * 0.953939
        ctx_2048 = 6.82029e-06 + 0.0200006 * (_ctx_2048t + 0.3 * jax.random.normal(jax.random.fold_in(_rk, 612), (4, 512, 512), jnp.float32))
        return (x, itok_BxS_13_99985, ctx_2048)
    x, itok_BxS_13_99985, ctx_2048 = _rec_inputs()

    def _L0_xattn_setup():
        import jax, jax.numpy as jnp
        import numpy as np
        B, S, D = (4, 1024, 512)
        E = 4
        F = 2048 // E
        VOCAB = 25000
        key = jax.random.key(seed)
        k1, k2, k3, k4, k5 = jax.random.split(key, 5)
        hidden_states = jax.random.normal(k1, (B, S, D), dtype=jnp.float32)
        token_ids = jax.random.randint(k2, (B, S), 0, VOCAB, dtype=jnp.int64)
        Wg = jax.random.normal(k3, (E, F, D), dtype=jnp.float32) * 0.02
        Wu = jax.random.normal(k4, (E, F, D), dtype=jnp.float32) * 0.02
        Wd = jax.random.normal(k5, (E, D, F), dtype=jnp.float32) * 0.02
        return {'hidden_states': hidden_states, 'token_ids': token_ids, 'Wg': Wg, 'Wu': Wu, 'Wd': Wd}
    _L0_xattn_all = _L0_xattn_setup()
    _L0_xattn_in = {k: v for k, v in _L0_xattn_all.items() if k in ()}
    del _L0_xattn_all

    def _L0_ffn_setup():
        import jax, jax.numpy as jnp
        import numpy as np
        EPS = 1e-05

        def _weight_quant(w):
            s = 1.0 / jnp.clip(jnp.mean(jnp.abs(w)), EPS, None)
            return jnp.clip(jnp.round(w * s), -1.0, 1.0) / s

        def _act_quant(x):
            s = 127.0 / jnp.clip(jnp.max(jnp.abs(x), axis=-1, keepdims=True), EPS, None)
            return jnp.clip(jnp.round(x * s), -128.0, 127.0) / s

        def bitlinear(x, w):
            wq = w + jax.lax.stop_gradient(_weight_quant(w) - w)
            xq = x + jax.lax.stop_gradient(_act_quant(x) - x)
            return xq @ wq.T
        key = jax.random.key(seed)
        k = jax.random.split(key, 5)
        B, S, H, E, D = (4, 1024, 512, 8, 512)
        x = jax.random.normal(k[0], (B, S, H), dtype=jnp.float32)
        router_w = jax.random.normal(k[1], (E, H), dtype=jnp.float32) * 0.02
        wg = jax.random.normal(k[2], (E, D, H), dtype=jnp.float32) * 0.02
        wu = jax.random.normal(k[3], (E, D, H), dtype=jnp.float32) * 0.02
        wd = jax.random.normal(k[4], (E, H, D), dtype=jnp.float32) * 0.02
        return {'x': x, 'router_w': router_w, 'wg': wg, 'wu': wu, 'wd': wd}
    _L0_ffn_all = _L0_ffn_setup()
    _L0_ffn_in = {k: v for k, v in _L0_ffn_all.items() if k in ('router_w', 'wg', 'wu', 'wd')}
    del _L0_ffn_all
    return {'x': x, 'itok_BxS_13_99985': itok_BxS_13_99985, 'ctx_2048': ctx_2048, 'L0_ffn_router_w': _L0_ffn_in['router_w'], 'L0_ffn_wg': _L0_ffn_in['wg'], 'L0_ffn_wu': _L0_ffn_in['wu'], 'L0_ffn_wd': _L0_ffn_in['wd']}

def reference(x, itok_BxS_13_99985, ctx_2048, L0_ffn_router_w, L0_ffn_wg, L0_ffn_wu, L0_ffn_wd):
    import jax
    import jax.numpy as jnp

    def _L0_xattn_ref(hidden_states, token_ids, Wg, Wu, Wd):
        import jax, jax.numpy as jnp
        import numpy as np
        B, S, D = (4, 1024, 512)
        E = 4
        F = 2048 // E
        VOCAB = 25000
        tokens_per_expert = VOCAB // E
        tid = jnp.clip(token_ids, 0, VOCAB - 1)
        expert_ids = jnp.minimum(tid // tokens_per_expert, E - 1)
        out = jnp.zeros_like(hidden_states)
        for e in range(E):
            g = jax.nn.silu(jnp.einsum('bsd,fd->bsf', hidden_states, Wg[e]))
            u = jnp.einsum('bsd,fd->bsf', hidden_states, Wu[e])
            y = jnp.einsum('bsf,df->bsd', g * u, Wd[e])
            out = jnp.where((expert_ids == e)[..., None], y, out)
        return out

    def _L0_ffn_ref(x, router_w, wg, wu, wd):
        import jax, jax.numpy as jnp
        import numpy as np
        EPS = 1e-05

        def _weight_quant(w):
            s = 1.0 / jnp.clip(jnp.mean(jnp.abs(w)), EPS, None)
            return jnp.clip(jnp.round(w * s), -1.0, 1.0) / s

        def _act_quant(x):
            s = 127.0 / jnp.clip(jnp.max(jnp.abs(x), axis=-1, keepdims=True), EPS, None)
            return jnp.clip(jnp.round(x * s), -128.0, 127.0) / s

        def bitlinear(x, w):
            wq = w + jax.lax.stop_gradient(_weight_quant(w) - w)
            xq = x + jax.lax.stop_gradient(_act_quant(x) - x)
            return xq @ wq.T
        B, S, H = x.shape
        E = wg.shape[0]
        logits = jnp.einsum('bsh,eh->bse', x, router_w)
        idx = jnp.argmax(logits, axis=-1).reshape(-1)
        xf = x.reshape(-1, H)
        out = jnp.zeros_like(xf)
        for e in range(E):
            g = bitlinear(xf, wg[e])
            u = bitlinear(xf, wu[e])
            y = bitlinear(jnp.square(jax.nn.relu(g)) * u, wd[e])
            out = out + jnp.where((idx == e)[:, None], y, 0.0)
        return out.reshape(B, S, H)
    x = x + _L0_xattn_ref(_layernorm(x, axis=-1), itok_BxS_13_99985, ctx_2048, ctx_2048, ctx_2048)
    x = x + _L0_ffn_ref(_layernorm(x, axis=-1), L0_ffn_router_w, L0_ffn_wg, L0_ffn_wu, L0_ffn_wd)
    return x

_drawn_inputs = setup_inputs


def setup_inputs(seed=0):
    import zlib

    import numpy as np

    out = dict(_drawn_inputs(seed))
    spreads = {}
    factors = {'L0_ffn_router_w': 6.173, 'L0_ffn_wg': 6.311, 'L0_ffn_wu': 5.761, 'L0_ffn_wd': 5.774}
    for name, (base, spread) in spreads.items():
        noise = np.random.default_rng([zlib.crc32(name.encode()), seed]).standard_normal(out[name].shape)
        drawn = base * np.exp(spread * noise) if base else spread * noise
        out[name] = jnp.asarray(drawn.astype(out[name].dtype))
    for name, factor in factors.items():
        out[name] = (out[name] * factor).astype(out[name].dtype)
    return out
```

```python
from contextlib import ExitStack

import concourse.bass as bass
from concourse import mybir

ALU = mybir.AluOpType
ACT = mybir.ActivationFunctionType
X = mybir.AxisListType.X
F32 = mybir.dt.float32
F32R = mybir.dt.float32r
BF16 = mybir.dt.bfloat16
F16 = mybir.dt.float16
I16 = mybir.dt.int16
I32 = mybir.dt.int32
U32 = mybir.dt.uint32

P = 128
N = 2048
D = 512
K = D // P
TILES = N // P
E1, E2 = 4, 8
B1 = TILES + E1 - 1
B2 = TILES + E2 - 1
MATS = 3 * E2
ID_STEP = 25000 // E1
EPS = 1e-5
QMAX = 127.0
MAGIC = 12582912.0
ROW = D + 4
SCALE_COL, OFFSET_COL, STEP_COL, CUBE_COL = range(D, D + 4)
EARLY = 5
MADE = 9
RING = 4


class At:

    def __init__(self, first, stride=0, turn=None):
        self.first, self.stride, self.turn = first, stride, turn

    def __add__(self, n):
        return At(self.first + n, self.stride, self.turn)

    def __sub__(self, n):
        return self + -n

    def __mul__(self, n):
        return At(self.first * n, self.stride * n, self.turn)

    def __floordiv__(self, n):
        assert self.stride % n == 0
        return At(self.first // n, self.stride // n, self.turn)

    def __mod__(self, n):
        assert self.stride % n == 0
        return self.first % n

    def __ge__(self, n):
        return self.first >= n

    @property
    def v(self):
        return self.first if self.turn is None else self.turn * self.stride + self.first

    def within(self, low, high, turns=1):
        if self.turn is not None:
            assert low <= self.first, (low, self.first)
            return True
        return low <= self.first < high


def run_ticks(eng, first, last, loop_first, unroll, turns, tick):
    for t in range(first, loop_first):
        tick(At(t))
    with eng.Fori(0, turns) as turn:
        for u in range(unroll):
            tick(At(loop_first + u, unroll, turn))
    for t in range(loop_first + unroll * turns, last + 1):
        tick(At(t))


T1_FIRST, T1_LAST, T1_LOOP, T1_UNROLL, T1_TURNS = -3, B1 + 2, 4, 4, 3
T2_FIRST, T2_LAST, T2_LOOP, T2_UNROLL, T2_TURNS = -2, B2 + 2, 4, 2, 8
assert T1_LOOP + T1_UNROLL * T1_TURNS + 3 <= B1
assert T2_LOOP + T2_UNROLL * T2_TURNS + 2 <= B2


def moe_program(nc, x_in, tokens_in, ctx_in, router_in, weights_in, out):
    with ExitStack() as whole:
        stack = [whole]

        def sb(name, shape, dt):
            return stack[-1].enter_context(nc.sbuf_tensor(name, shape, dt))

        def sem(name):
            return whole.enter_context(nc.semaphore(name))

        x1_rows = nc.dram_tensor("x1_rows", [N, ROW], F32).ap()

        bank = [whole.enter_context(nc.psum_tensor(f"bank{i}", [P, D], F32)) for i in range(8)]

        ternary = sb("ternary", [P, MATS * K * D], BF16)
        ident = sb("ident", [P, P], F32)
        before = sb("before", [P, P], F32)
        ones = sb("ones", [P, P], F32)
        iota_i = sb("iota_i", [P, P], I32)
        iota = sb("iota", [P, P], F32)
        minus_half = sb("minus_half", [P, 1], F32)
        token1 = sb("token1", [P, TILES], F32)
        token1_i = sb("token1_i", [P, TILES], I32)
        token_ids = sb("token_ids", [P, TILES], I32)
        at_least = sb("at_least", [P, (E1 + 1) * TILES], F32)
        member1 = sb("member1", [P, E1 * TILES], F32)
        member2 = sb("member2", [P, E2 * B1], F32)
        scan = sb("scan", [P, E2 * B1], F32)
        earlier = sb("earlier", [P, E2 * B1], F32)
        placed = sb("placed", [P, E2 * B1], F32)
        place = sb("place", [P, B1], F32)
        place_block = sb("place_block", [P, B1], F32)
        place_row = sb("place_row", [P, B1], F32)
        small = sb("small", [P, 10, E2], F32)
        row_hot = sb("row_hot", [P, RING, P], F16)
        block_hot = sb("block_hot", [P, RING, B2], F16)
        table1 = sb("table1", [P, B1], F32)
        table2 = sb("table2", [P, B2], F32)
        valid1 = sb("valid1", [P, B1], F32)
        pad = sb("pad", [P, B2], F32)
        gather1 = sb("gather1", [P, B1], I32)
        store1 = sb("store1", [P, B1], I32)
        gather2 = sb("gather2", [P, B2], I32)
        store2 = sb("store2", [P, B2], I32)
        expert_f = sb("expert_f", [P, B2], F32)
        expert1 = sb("expert1", [P, B1], I32)
        expert2 = sb("expert2", [P, B2], I32)
        router = sb("router", [P, K * E2], F32)
        abs_sum = sb("abs_sum", [P, MATS], F32)
        w_mean = sb("w_mean", [P, MATS], F32)
        w_scale = sb("w_scale", [P, MATS], F32)

        inputs_in = sem("inputs_in")
        made = sem("made")
        pool_passed, dve_passed, pe_passed = sem("pool_passed"), sem("dve_passed"), sem("pe_passed")
        sorting = sem("sorting")
        sort_pe = sem("sort_pe")
        hot_ready = sem("hot_ready")
        hot_used = sem("hot_used")

        def sort_vector(dve, link, member, n_exp, n_tiles, n_blocks, tokens, table, experts, gather, store, lap):
            width = n_exp * n_tiles
            m = member[:, 0:width]
            m3 = m.rearrange("p (e t) -> p e t", e=n_exp)
            cnt, blocks, blocks_sum, cnt_sum, start, base, lift, part = (small[:, i, 0:n_exp] for i in range(8))
            link(dve.tensor_tensor_scan(scan[:, 0:width], ones_wide[:, 0:width], m, 0.0, ALU.mult, ALU.add))
            link(dve.tensor_tensor(earlier[:, 0:width], scan[:, 0:width], m, ALU.subtract))
            link(dve.tensor_reduce(part, m3, X, ALU.add))
            dve.sem_inc(sorting, 1)
            dve.wait_ge(sort_pe, 2 * lap + 1)
            link(dve.tensor_copy(cnt, bank[7][:, 256:256 + n_exp]))
            link(dve.tensor_scalar(blocks, cnt, 1.0 / P, 0.5 - 0.5 / P, ALU.mult, ALU.add))
            link(dve.tensor_scalar(blocks, blocks, MAGIC, MAGIC, ALU.add, ALU.subtract))
            link(dve.tensor_tensor_scan(blocks_sum, ones[:, 0:n_exp], blocks, 0.0, ALU.mult, ALU.add))
            link(dve.tensor_tensor_scan(cnt_sum, ones[:, 0:n_exp], cnt, 0.0, ALU.mult, ALU.add))
            link(dve.tensor_tensor(start, blocks_sum, blocks, ALU.subtract))
            link(dve.tensor_tensor(base, cnt_sum, cnt, ALU.subtract))
            link(dve.scalar_tensor_tensor(lift, start, float(P), base, ALU.mult, ALU.subtract))
            for e in range(n_exp):
                cols = slice(e * n_tiles, (e + 1) * n_tiles)
                last = dve.scalar_tensor_tensor(placed[:, cols], bank[7][:, cols], lift[:, e:e + 1], member[:, cols],
                                                ALU.add, ALU.mult)
            link(last)
            link(dve.tensor_reduce(place[:, 0:n_tiles], placed[:, 0:width].rearrange("p (e t) -> p t e", e=n_exp),
                                   X, ALU.add))
            link(dve.tensor_scalar(place_block[:, 0:n_tiles], place[:, 0:n_tiles], 1.0 / P, 0.5 / P - 0.5,
                                   ALU.mult, ALU.add))
            link(dve.tensor_scalar(place_block[:, 0:n_tiles], place_block[:, 0:n_tiles], MAGIC, MAGIC,
                                   ALU.add, ALU.subtract))
            link(dve.scalar_tensor_tensor(place_row[:, 0:n_tiles], place_block[:, 0:n_tiles], -float(P),
                                          place[:, 0:n_tiles], ALU.mult, ALU.add))
            for t in range(n_tiles):
                if t >= RING:
                    dve.wait_ge(hot_used, lap * TILES + t - RING + 1)
                dve.tensor_scalar(row_hot[:, t % RING, :], iota[:, 0:P], place_row[:, t:t + 1], None, ALU.is_equal)
                dve.tensor_scalar(block_hot[:, t % RING, 0:n_blocks], iota[:, 0:n_blocks], place_block[:, t:t + 1],
                                  tokens[:, t:t + 1], ALU.is_equal, ALU.mult).then_inc(hot_ready, 1)
            link(dve.tensor_scalar(expert_f[:, 0:n_blocks], iota[:, 0:n_blocks], start[:, 1:2], None, ALU.is_ge))
            for e in range(2, n_exp):
                link(dve.scalar_tensor_tensor(expert_f[:, 0:n_blocks], iota[:, 0:n_blocks], start[:, e:e + 1],
                                              expert_f[:, 0:n_blocks], ALU.is_ge, ALU.add))
            link(dve.tensor_copy(experts[:, 0:n_blocks], expert_f[:, 0:n_blocks]))
            dve.wait_ge(sort_pe, 2 * lap + 2)
            link(dve.tensor_copy(table[:, 0:n_blocks], bank[6][:, 0:n_blocks]))
            link(dve.tensor_scalar(pad[:, 0:n_blocks], table[:, 0:n_blocks], 0.0, None, ALU.is_equal))
            dve.scalar_tensor_tensor(gather[:, 0:n_blocks], table[:, 0:n_blocks], -1.0, pad[:, 0:n_blocks],
                                     ALU.add, ALU.add)
            link(dve.scalar_tensor_tensor(pad[:, 0:n_blocks], pad[:, 0:n_blocks], float(2 * N), table[:, 0:n_blocks],
                                          ALU.mult, ALU.add))
            link(dve.tensor_scalar(store[:, 0:n_blocks], pad[:, 0:n_blocks], -1.0, None, ALU.add))

        def sort_tensor(pe, member, n_exp, n_tiles, n_blocks, lap):
            width = n_exp * n_tiles
            pe.wait_ge(sorting, lap + 1)
            pe.matmul(bank[7][:, 0:width], before[:, :], member[:, 0:width], start=True, stop=False)
            pe.matmul(bank[7][:, 0:width], ones[:, 0:P], earlier[:, 0:width], start=False, stop=True)
            pe.matmul(bank[7][:, 256:256 + n_exp], ones[:, 0:P], small[:, 7, 0:n_exp], start=True,
                      stop=True).then_inc(sort_pe, 1)
            for t in range(n_tiles):
                pe.wait_ge(hot_ready, lap * TILES + t + 1)
                last = pe.matmul(bank[6][:, 0:n_blocks], row_hot[:, t % RING, :], block_hot[:, t % RING, 0:n_blocks],
                                 start=(t == 0), stop=(t == n_tiles - 1))
                last.then_inc(hot_used, 1)
            pe.drain().then_inc(sort_pe, 1)

        ones_wide = sb("ones_wide", [P, E2 * B1], F32)

        with ExitStack() as inner:
            stack.append(inner)
            ctx_hi = sb("ctx_hi", [P, E1 * K * D], F32R)
            ctx_lo = sb("ctx_lo", [P, E1 * K * D], F32R)
            staged = [sb(f"staged{i}", [P, K * D], F32) for i in range(2)]
            x = [sb(f"x{i}", [P, D], F32) for i in range(RING)]
            h = sb("h", [P, D], F32)
            hT_hi = sb("hT_hi", [P, D], F32R)
            hT_lo = sb("hT_lo", [P, D], F32R)
            sil = sb("sil", [P, D], F32)
            p = sb("p", [P, D], F32)
            pT_hi = sb("pT_hi", [P, D], F32R)
            pT_lo = sb("pT_lo", [P, D], F32R)
            row = [sb(f"row{i}", [P, ROW], F32) for i in range(2)]
            z = sb("z", [P, D], F32)
            zT = sb("zT", [P, D], F32)
            stats1 = sb("stats1", [P, 6], F32)
            stats2 = sb("stats2", [P, 6], F32)
            mv1 = [sb(f"mv1_{i}", [P, 2], F32) for i in range(2)]
            mv2 = [sb(f"mv2_{i}", [P, 3], F32) for i in range(2)]
            ln1 = [sb(f"ln1_{i}", [P, 3], F32) for i in range(2)]
            ln2 = [sb(f"ln2_{i}", [P, 6], F32) for i in range(2)]
            best = sb("best", [P, 8], F32)
            best_at = sb("best_at", [P, 8], U32)
            choice = sb("choice", [P, 1], F32)
            gather_at = [sb(f"gather_at{i}", [P, 1], I32) for i in range(RING)]
            store_at = [sb(f"store_at{i}", [P, 1], I32) for i in range(2)]

            staged_in = [sem(f"staged_in{i}") for i in range(2)]
            ctx_hi_ready, ctx_lo_ready = sem("ctx_hi_ready"), sem("ctx_lo_ready")
            sorted1 = sem("sorted1")
            gather_at_ready, store_at_ready = sem("gather_at_ready"), sem("store_at_ready")
            x_in_sem = [sem(f"x_in{i}") for i in range(RING)]
            moments1 = sem("moments1")
            norm1 = sem("norm1")
            h_ready, hT_ready, hT_hi_ready, hT_lo_ready = (sem(n) for n in ("h_ready", "hT_ready", "hT_hi_ready", "hT_lo_ready"))
            a_ready, sil_ready, p_ready = (sem(n) for n in ("a_ready", "sil_ready", "p_ready"))
            pT_ready, pT_hi_ready, pT_lo_ready = (sem(n) for n in ("pT_ready", "pT_hi_ready", "pT_lo_ready"))
            y_ready, x1_ready, moments2, norm2 = (sem(n) for n in ("y_ready", "x1_ready", "moments2", "norm2"))
            z_ready, zT_ready, zT_copied, logits_ready = (sem(n) for n in ("z_ready", "zT_ready", "zT_copied", "logits_ready"))
            zmax_ready, step_ready, step_inv, quant_ready = (sem(n) for n in ("zmax_ready", "step_ready", "step_inv", "quant_ready"))
            routed = sem("routed")
            row_out = [sem(f"row_out{i}") for i in range(2)]
            abs_ready, mean_ready, tern = sem("abs_ready"), sem("mean_ready"), sem("tern")

            hT_ps, pT_ps, zT_ps, y_ps = bank[0], bank[1], bank[2], bank[3]
            a_ps = [bank[4], bank[5]]
            mean_ps, logits_ps = bank[6], bank[7]

            with nc.Block() as block:

                @block.sync
                def _(sp):
                    sp.dma_start(token_ids[:, :], tokens_in).then_inc(inputs_in, 16)
                    sp.dma_start(router[:, :], router_in).then_inc(inputs_in, 16)
                    for e in range(E1):
                        if e >= 2:
                            sp.wait_ge(ctx_lo_ready, e - 1)
                        sp.dma_start(staged[e % 2][:, :], ctx_in[e]).then_inc(staged_in[e % 2], 16)

                    def load(m):
                        if m >= 2:
                            sp.wait_ge(tern, (m * 4 - 5).v)
                        sp.dma_start(staged[m % 2][:, :], weights_in[bass.ds(m.v, 1)].rearrange("a p n -> (a p) n"))\
                          .then_inc(staged_in[m % 2], 16)

                    for e in range(2):
                        sp.wait_ge(ctx_lo_ready, E1 - 1 + e)
                        load(At(e))
                    with sp.Fori(0, MATS // 2 - 1) as turn:
                        for u in range(2):
                            load(At(2 + u, 2, turn))

                @block.gpsimd
                def _(pool):
                    pool.iota(iota_i[:, :], [[1, P]], base=0, channel_multiplier=0).then_inc(made, 1)
                    pool.iota(token1_i[:, :], [[P, TILES]], base=1, channel_multiplier=1).then_inc(made, 1)
                    pool.memset(ones[:, :], 1.0).then_inc(made, 1)
                    pool.memset(ones_wide[:, :], 1.0).then_inc(made, 1)
                    pool.memset(before[:, :], 0.0).then_inc(made, 1)
                    pool.memset(ident[:, :], 0.0).then_inc(made, 1)
                    pool.memset(minus_half[:, :], -0.5).then_inc(made, 1)
                    pool.wait_ge(made, 7)
                    pool.affine_select(before[:, :], before[:, :], [[-1, P]], ALU.is_ge, 1.0, base=0,
                                       channel_multiplier=1).then_inc(made, 1)
                    pool.affine_select(ident[:, :], ident[:, :], [[-1, P]], ALU.not_equal, 1.0, base=0,
                                       channel_multiplier=1).then_inc(made, 1)

                    def tick(t):
                        b = t + 2
                        if b.within(0, B1):
                            s = ln1[b % 2]
                            if b >= 2:
                                pool.wait_ge(h_ready, (b - 1).v)
                            pool.wait_ge(moments1, (b * 2 + 2).v)
                            pool.sem_inc(pool_passed, 1)
                            pool.tensor_scalar(s[:, 0:1], mv1[b % 2][:, 1:2], EPS, None, ALU.add).then_inc(norm1, 1)
                            pool.wait_ge(norm1, (b * 3 + 1).v)
                            pool.sem_inc(pool_passed, 1)
                            pool.tensor_tensor(s[:, 1:2], s[:, 0:1], minus_half[:, :], ALU.pow).then_inc(norm1, 1)
                            pool.wait_ge(norm1, (b * 3 + 2).v)
                            pool.sem_inc(pool_passed, 1)
                            pool.tensor_scalar(s[:, 2:3], mv1[b % 2][:, 0:1], s[:, 1:2], -1.0, ALU.mult, ALU.mult)\
                                .then_inc(norm1, 1)
                        b = t - 2
                        if b.within(0, B1):
                            s, r = ln2[b % 2], row[b % 2]
                            pool.wait_ge(step_inv, (b + 1).v)
                            pool.sem_inc(pool_passed, 1)
                            pool.tensor_scalar(r[:, SCALE_COL:SCALE_COL + 1], s[:, 1:2], s[:, 4:5], None, ALU.mult)\
                                .then_inc(quant_ready, 1)
                            pool.wait_ge(quant_ready, (b * 3 + 1).v)
                            pool.sem_inc(pool_passed, 1)
                            pool.tensor_scalar(r[:, OFFSET_COL:OFFSET_COL + 1], r[:, SCALE_COL:SCALE_COL + 1],
                                               mv2[b % 2][:, 2:3], None, ALU.mult).then_inc(quant_ready, 1)
                            st = r[:, STEP_COL:STEP_COL + 1]
                            pool.tensor_scalar(r[:, CUBE_COL:CUBE_COL + 1], st, st, st, ALU.mult, ALU.mult)\
                                .then_inc(quant_ready, 1)
                            if b >= 2:
                                pool.wait_ge(row_out[b % 2], ((b // 2) * 16).v)
                            pool.sem_inc(pool_passed, 1)
                            pool.tensor_copy(store_at[b % 2][:, :], store1[:, bass.ds(b.v, 1)])\
                                .then_inc(store_at_ready, 1)
                            pool.wait_ge(store_at_ready, (b + 1).v)
                            pool.wait_ge(quant_ready, (b * 3 + 3).v)
                            pool.sem_inc(pool_passed, 1)
                            pool.indirect_dma_start(x1_rows, bass.IndirectOffsetOnAxis(ap=store_at[b % 2][:, :], axis=0),
                                                    r[:, :], None, bounds_check=N - 1, oob_is_err=False)\
                                .then_inc(row_out[b % 2], 16)
                        b = t - 1
                        if b.within(0, B1):
                            s = ln2[b % 2]
                            pool.wait_ge(moments2, (b * 3 + 3).v)
                            pool.sem_inc(pool_passed, 1)
                            pool.tensor_scalar(s[:, 0:1], mv2[b % 2][:, 1:2], EPS, None, ALU.add).then_inc(norm2, 1)
                            pool.wait_ge(norm2, (b * 2 + 1).v)
                            pool.sem_inc(pool_passed, 1)
                            pool.tensor_tensor(s[:, 1:2], s[:, 0:1], minus_half[:, :], ALU.pow).then_inc(norm2, 1)
                            pool.wait_ge(norm2, (b * 2 + 2).v)
                            pool.wait_ge(zmax_ready, (b + 1).v)
                            pool.sem_inc(pool_passed, 1)
                            pool.tensor_scalar(s[:, 3:4], s[:, 2:3], s[:, 1:2], None, ALU.mult).then_inc(step_ready, 1)
                            pool.wait_ge(step_ready, (b * 2 + 1).v)
                            pool.sem_inc(pool_passed, 1)
                            pool.tensor_scalar(row[b % 2][:, STEP_COL:STEP_COL + 1], s[:, 3:4], EPS, 1.0 / QMAX,
                                               ALU.max, ALU.mult).then_inc(step_ready, 1)
                        b = t + 3
                        if b.within(0, B1):
                            if b >= RING:
                                pool.wait_ge(x1_ready, (b - (RING - 1)).v)
                            pool.sem_inc(pool_passed, 1)
                            pool.tensor_copy(gather_at[b % RING][:, :], gather1[:, bass.ds(b.v, 1)])\
                                .then_inc(gather_at_ready, 1)
                            pool.wait_ge(gather_at_ready, (b + 1).v)
                            pool.sem_inc(pool_passed, 1)
                            pool.indirect_dma_start(x[b % RING][:, :], None, x_in,
                                                    bass.IndirectOffsetOnAxis(ap=gather_at[b % RING][:, :], axis=0),
                                                    bounds_check=N - 1, oob_is_err=False)\
                                .then_inc(x_in_sem[b % RING], 16)

                    pool.wait_ge(sorted1, 1)
                    run_ticks(pool, T1_FIRST, T1_LAST, T1_LOOP, T1_UNROLL, T1_TURNS, tick)
                    for i in range(2):
                        pool.wait_ge(row_out[i], 16 * ((B1 - i + 1) // 2))

                @block.scalar
                def _(act):
                    act.preload_act_table(ACT.Silu)
                    for e in range(E1):
                        act.wait_ge(staged_in[e % 2], 16 * (e // 2 + 1))
                        nc.scalar.activation(ctx_hi[:, e * K * D:(e + 1) * K * D], staged[e % 2][:, :], ACT.Copy)\
                            .then_inc(ctx_hi_ready, 1)

                    def sum_abs(m):
                        act.wait_ge(staged_in[m % 2], ((m // 2) * 16 + 16 * (E1 // 2 + 1)).v)
                        nc.scalar.activation(ternary[:, bass.ds((m * (K * D)).v, K * D)], staged[m % 2][:, :], ACT.Abs,
                                             accum_out=abs_sum[:, bass.ds(m.v, 1)]).then_inc(abs_ready, 1)

                    def tick(t):
                        b = t - 1
                        if b.within(0, B1):
                            act.wait_ge(pT_ready, (b + 1).v)
                            nc.scalar.activation(pT_hi[:, :], pT_ps[:, :], ACT.Copy).then_inc(pT_hi_ready, 1)
                        b = t - 2
                        if b.within(0, B1):
                            act.wait_ge(zT_ready, (b + 1).v)
                            if b >= 1:
                                act.wait_ge(logits_ready, b.v)
                            nc.scalar.activation(zT[:, :], zT_ps[:, :], ACT.Copy).then_inc(zT_copied, 1)
                        m = t + (3 + EARLY)
                        if m.within(EARLY, MATS):
                            sum_abs(m)
                        b = t + 1
                        if b.within(0, B1):
                            act.wait_ge(hT_ready, (b + 1).v)
                            if b >= 1:
                                act.wait_ge(a_ready, b.v)
                            nc.scalar.activation(hT_hi[:, :], hT_ps[:, :], ACT.Copy).then_inc(hT_hi_ready, 1)
                        b = t
                        if b.within(0, B1):
                            act.wait_ge(a_ready, (b + 1).v)
                            if b >= 1:
                                act.wait_ge(p_ready, b.v)
                            nc.scalar.activation(sil[:, :], a_ps[b % 2][:, :], ACT.Silu).then_inc(sil_ready, 1)
                        b = t + 2
                        if b.within(0, B1):
                            act.wait_ge(norm1, (b * 3 + 3).v)
                            if b >= 1:
                                act.wait_ge(hT_ready, b.v)
                            s = ln1[b % 2]
                            nc.scalar.activation(h[:, :], x[b % RING][:, :], ACT.Identity, bias=s[:, 2:3],
                                                 scale=s[:, 1:2]).then_inc(h_ready, 1)
                        b = t - 1
                        if b.within(0, B1):
                            act.wait_ge(moments2, (b * 3 + 3).v)
                            if b >= 1:
                                act.wait_ge(zT_ready, b.v)
                                act.wait_ge(zmax_ready, b.v)
                            nc.scalar.activation(z[:, :], row[b % 2][:, 0:D], ACT.Identity, bias=mv2[b % 2][:, 2:3])\
                                .then_inc(z_ready, 1)

                    for m in range(EARLY):
                        sum_abs(At(m))
                    run_ticks(act, T1_FIRST, T1_LAST, T1_LOOP, T1_UNROLL, T1_TURNS, tick)

                @block.vector
                def _(dve):
                    chain = sem("chain1")
                    count = [0]

                    def link(ins):
                        count[0] += 1
                        ins.then_inc(chain, 1)
                        dve.wait_ge(chain, count[0])

                    dve.wait_ge(made, MADE)
                    dve.wait_ge(inputs_in, 32)
                    link(dve.tensor_copy(iota[:, :], iota_i[:, :]))
                    link(dve.tensor_copy(token1[:, :], token1_i[:, :]))
                    dve.memset(at_least[:, 0:TILES], 1.0)
                    dve.memset(at_least[:, E1 * TILES:], 0.0)
                    for e in range(1, E1):
                        last = dve.tensor_scalar(at_least[:, e * TILES:(e + 1) * TILES], token_ids[:, :],
                                                 float(e * ID_STEP), None, ALU.is_ge)
                    link(last)
                    link(dve.tensor_tensor(member1[:, :], at_least[:, 0:E1 * TILES], at_least[:, TILES:], ALU.subtract))
                    sort_vector(dve, link, member1, E1, TILES, B1, token1, table1, expert1, gather1, store1, 0)
                    link(dve.tensor_scalar(valid1[:, :], table1[:, :], 0.0, None, ALU.is_gt))
                    dve.sem_inc(sorted1, 1)
                    for e in range(E1):
                        cols = slice(e * K * D, (e + 1) * K * D)
                        dve.wait_ge(ctx_hi_ready, e + 1)
                        dve.tensor_tensor(ctx_lo[:, cols], staged[e % 2][:, :], ctx_hi[:, cols].bitcast(F32),
                                          ALU.subtract).then_inc(ctx_lo_ready, 1)

                    def ternarize(m):
                        cols = bass.ds((m * (K * D)).v, K * D)
                        one = bass.ds(m.v, 1)
                        dve.wait_ge(mean_ready, (m + 1).v)
                        dve.tensor_scalar(w_mean[:, one], mean_ps[:, bass.ds((m + 64).v, 1)], 1.0 / (D * D), EPS,
                                          ALU.mult, ALU.max).then_inc(tern, 1)
                        dve.wait_ge(tern, (m * 4 + 1).v)
                        dve.reciprocal(w_scale[:, one], w_mean[:, one]).then_inc(tern, 1)
                        dve.wait_ge(tern, (m * 4 + 2).v)
                        dve.tensor_scalar(ternary[:, cols].bitcast(I16), staged[m % 2][:, :], w_scale[:, one], -1.0,
                                          ALU.mult, ALU.max).then_inc(tern, 1)
                        dve.wait_ge(tern, (m * 4 + 3).v)
                        dve.tensor_scalar(ternary[:, cols], ternary[:, cols].bitcast(I16), 1.0, None,
                                          ALU.min).then_inc(tern, 1)

                    def tick(t):
                        b = t - 2
                        if b.within(0, B1):
                            dve.wait_ge(step_ready, (b * 2 + 2).v)
                            dve.reciprocal(ln2[b % 2][:, 4:5], row[b % 2][:, STEP_COL:STEP_COL + 1]).then_inc(step_inv, 1)
                        b = t + 2
                        if b.within(0, B1):
                            dve.wait_ge(x_in_sem[b % RING], ((b // RING) * 16 + 16).v)
                            dve.bn_stats(stats1[:, :], x[b % RING][:, :]).then_inc(moments1, 1)
                            dve.wait_ge(moments1, (b * 2 + 1).v)
                            if b >= 2:
                                dve.wait_ge(norm1, (b * 3 - 3).v)
                            dve.sem_inc(dve_passed, 1)
                            dve.bn_aggr(mv1[b % 2][:, :], stats1[:, :]).then_inc(moments1, 1)
                        b = t - 1
                        if b.within(0, B1):
                            dve.wait_ge(pT_hi_ready, (b + 1).v)
                            if b >= 1:
                                dve.wait_ge(y_ready, b.v)
                            dve.tensor_tensor(pT_lo[:, :], pT_ps[:, :], pT_hi[:, :].bitcast(F32), ALU.subtract)\
                                .then_inc(pT_lo_ready, 1)
                        m = t + (2 + EARLY)
                        if m.within(EARLY, MATS):
                            ternarize(m)
                        b = t + 1
                        if b.within(0, B1):
                            dve.wait_ge(hT_hi_ready, (b + 1).v)
                            dve.tensor_tensor(hT_lo[:, :], hT_ps[:, :], hT_hi[:, :].bitcast(F32), ALU.subtract)\
                                .then_inc(hT_lo_ready, 1)
                        b = t
                        if b.within(0, B1):
                            dve.wait_ge(sil_ready, (b + 1).v)
                            if b >= 1:
                                dve.wait_ge(pT_ready, b.v)
                            dve.tensor_tensor(p[:, :], a_ps[b % 2][:, :], sil[:, :], ALU.mult).then_inc(p_ready, 1)
                        b = t - 2
                        if b.within(0, B1):
                            dve.wait_ge(logits_ready, (b + 1).v)
                            dve.sem_inc(dve_passed, 1)
                            dve.max(best[:, :], logits_ps[:, 0:E2]).then_inc(routed, 1)
                            dve.wait_ge(routed, (b * 4 + 1).v)
                            dve.sem_inc(dve_passed, 1)
                            dve.max_index(best_at[:, :], best[:, :], logits_ps[:, 0:E2]).then_inc(routed, 1)
                            dve.wait_ge(routed, (b * 4 + 2).v)
                            dve.tensor_copy(choice[:, :], best_at[:, 0:1]).then_inc(routed, 1)
                            dve.wait_ge(routed, (b * 4 + 3).v)
                            m2 = member2[:, :].rearrange("p (e t) -> p e t", e=E2)[:, :, bass.ds(b.v, 1)]
                            dve.tensor_scalar(m2, iota[:, 0:E2].rearrange("p (e a) -> p e a", a=1), choice[:, :],
                                              valid1[:, bass.ds(b.v, 1)], ALU.is_equal, ALU.mult).then_inc(routed, 1)
                        b = t - 1
                        if b.within(0, B1):
                            r = row[b % 2]
                            dve.wait_ge(y_ready, (b + 1).v)
                            if b >= 2:
                                dve.wait_ge(row_out[b % 2], ((b // 2) * 16).v)
                            dve.tensor_tensor(r[:, 0:D], y_ps[:, :], x[b % RING][:, :], ALU.add).then_inc(x1_ready, 1)
                            dve.wait_ge(x1_ready, (b + 1).v)
                            dve.bn_stats(stats2[:, :], r[:, 0:D]).then_inc(moments2, 1)
                            dve.wait_ge(moments2, (b * 3 + 1).v)
                            dve.sem_inc(dve_passed, 1)
                            dve.bn_aggr(mv2[b % 2][:, 0:2], stats2[:, :]).then_inc(moments2, 1)
                            dve.wait_ge(moments2, (b * 3 + 2).v)
                            dve.tensor_scalar(mv2[b % 2][:, 2:3], mv2[b % 2][:, 0:1], -1.0, None, ALU.mult)\
                                .then_inc(moments2, 1)
                            dve.wait_ge(z_ready, (b + 1).v)
                            dve.tensor_reduce(ln2[b % 2][:, 2:3], z[:, :], X, ALU.max, apply_absolute_value=True)\
                                .then_inc(zmax_ready, 1)

                    for m in range(EARLY):
                        ternarize(At(m))
                    run_ticks(dve, T1_FIRST, T1_LAST, T1_LOOP, T1_UNROLL, T1_TURNS, tick)

                @block.tensor
                def _(pe):
                    pe.wait_ge(made, MADE)
                    sort_tensor(pe, member1, E1, TILES, B1, 0)

                    def sum_mean(m):
                        pe.wait_ge(abs_ready, (m + 1).v)
                        if m >= 1:
                            pe.wait_ge(tern, (m * 4 - 3).v)
                        pe.matmul(mean_ps[:, bass.ds((m + 64).v, 1)], ones[:, 0:P], abs_sum[:, bass.ds(m.v, 1)],
                                  start=True, stop=True).then_inc(mean_ready, 1)

                    def transpose(ps, src):
                        for k in range(K):
                            last = pe.transpose(ps[:, k * P:(k + 1) * P], src[:, k * P:(k + 1) * P], ident[:, :])
                        return last

                    def expert_of(b):
                        return pe.value_load(expert1[0:1, bass.ds(b.v, 1)], min_val=0, max_val=E1 - 1)

                    def product(ps, hi, lo, e):
                        pairs = [(hi, ctx_hi), (hi, ctx_lo), (lo, ctx_hi)]
                        for n, (left, right) in enumerate(pairs):
                            for k in range(K):
                                last = pe.matmul(ps[:, :], left[:, k * P:(k + 1) * P],
                                                 right[:, bass.ds(e * (K * D) + k * D, D)],
                                                 start=(n == 0 and k == 0), stop=(n == 2 and k == K - 1))
                        return last

                    def tick(t):
                        b = t - 1
                        if b.within(0, B1):
                            pe.wait_ge(p_ready, (b + 1).v)
                            if b >= 1:
                                pe.wait_ge(pT_lo_ready, b.v)
                            transpose(pT_ps, p).then_inc(pT_ready, 1)
                        b = t - 2
                        if b.within(0, B1):
                            pe.wait_ge(z_ready, (b + 1).v)
                            if b >= 1:
                                pe.wait_ge(zT_copied, b.v)
                            transpose(zT_ps, z).then_inc(zT_ready, 1)
                        m = t + (2 + EARLY)
                        if m.within(EARLY, MATS):
                            sum_mean(m)
                        b = t
                        if b.within(0, B1):
                            e = expert_of(b)
                            pe.wait_ge(hT_lo_ready, (b + 1).v)
                            if b >= 2:
                                pe.wait_ge(p_ready, (b - 1).v)
                            product(a_ps[b % 2], hT_hi, hT_lo, e).then_inc(a_ready, 1)
                        b = t - 2
                        if b.within(0, B1):
                            pe.wait_ge(zT_copied, (b + 1).v)
                            if b >= 1:
                                pe.wait_ge(routed, (b * 4).v)
                            for k in range(K):
                                last = pe.matmul(logits_ps[:, 0:E2], zT[:, k * P:(k + 1) * P],
                                                 router[:, k * E2:(k + 1) * E2], start=(k == 0), stop=(k == K - 1))
                            last.then_inc(logits_ready, 1)
                        b = t + 1
                        if b.within(0, B1):
                            pe.wait_ge(h_ready, (b + 1).v)
                            if b >= 1:
                                pe.wait_ge(hT_lo_ready, b.v)
                            transpose(hT_ps, h).then_inc(hT_ready, 1)
                        b = t - 1
                        if b.within(0, B1):
                            e = expert_of(b)
                            pe.wait_ge(pT_lo_ready, (b + 1).v)
                            if b >= 1:
                                pe.wait_ge(x1_ready, b.v)
                            product(y_ps, pT_hi, pT_lo, e).then_inc(y_ready, 1)

                    for m in range(EARLY):
                        sum_mean(At(m))
                    pe.wait_ge(ctx_lo_ready, E1)
                    pe.wait_ge(sorted1, 1)
                    run_ticks(pe, T1_FIRST, T1_LAST, T1_LOOP, T1_UNROLL, T1_TURNS, tick)

            stack.pop()

        with ExitStack() as inner:
            stack.append(inner)
            x1 = sb("x1_slots", [P, B2 * ROW], F32)
            t8 = sb("t8", [P, D], F32)
            qT = sb("qT", [P, D], BF16)
            relu = sb("relu", [P, D], F32)
            relu2 = sb("relu2", [P, D], F32)
            prod = [sb(f"prod{i}", [P, D], F32) for i in range(2)]
            r8 = sb("r8", [P, D], F32)
            rT = sb("rT", [P, D], BF16)
            fac = [sb(f"fac{i}", [P, 6], F32) for i in range(2)]
            magic = sb("magic", [P, 1], F32)
            gu_mean = sb("gu_mean", [P, E2], F32)
            gu_block = sb("gu_block", [P, B2], F32)
            d_block = sb("d_block", [P, B2], F32)
            out_scale = sb("out_scale", [P, B2], F32)
            is_expert = sb("is_expert", [P, B2], F32)

            sorted2 = sem("sorted2")
            x1_in = [sem(f"x1_in{i}") for i in range(2)]
            t8_ready, tT_ready, qT_ready = (sem(n) for n in ("t8_ready", "tT_ready", "qT_ready"))
            g_ready, u_ready, relu_ready, relu2_ready = (sem(n) for n in ("g_ready", "u_ready", "relu_ready", "relu2_ready"))
            prod_ready, factors, r8_ready, rT_ps_ready, rT_ready = (
                sem(n) for n in ("prod_ready", "factors", "r8_ready", "rT_ps_ready", "rT_ready"))
            d_ready, out_ready, out_done = sem("d_ready"), sem("out_ready"), sem("out_done")

            g_ps, u_ps = [bank[0], bank[1]], [bank[2], bank[3]]
            tT_ps, rT_ps, d_ps = bank[4], bank[5], bank[6]

            def row_of(b, first, n):
                return x1[:, bass.ds((b * ROW + first).v, n)]

            with nc.Block() as block:

                @block.gpsimd
                def _(pool):
                    pool.wait_ge(sorted2, 1)
                    for b in range(B2):
                        if b >= 2:
                            pool.wait_ge(x1_in[b % 2], 16 * (b // 2))
                        pool.indirect_dma_start(x1[:, b * ROW:(b + 1) * ROW], None, x1_rows,
                                                bass.IndirectOffsetOnAxis(ap=gather2[:, b:b + 1], axis=0),
                                                bounds_check=N - 1, oob_is_err=False).then_inc(x1_in[b % 2], 16)
                    for b in range(B2):
                        pool.wait_ge(out_ready, b + 1)
                        pool.indirect_dma_start(out, bass.IndirectOffsetOnAxis(ap=store2[:, b:b + 1], axis=0),
                                                x1[:, b * ROW:b * ROW + D], None,
                                                bounds_check=N - 1, oob_is_err=False).then_inc(out_done, 16)
                    pool.wait_ge(out_done, 16 * B2)

                @block.scalar
                def _(act):
                    def tick(t):
                        b = t - 2
                        if b.within(0, B2):
                            act.wait_ge(rT_ps_ready, (b + 1).v)
                            if b >= 1:
                                act.wait_ge(d_ready, b.v)
                            nc.scalar.activation(rT[:, :], rT_ps[:, :], ACT.Copy, bias=-MAGIC).then_inc(rT_ready, 1)
                        b = t - 1
                        if b.within(0, B2):
                            act.wait_ge(factors, (b * 6 + 6).v)
                            if b >= 1:
                                act.wait_ge(rT_ps_ready, b.v)
                            nc.scalar.activation(r8[:, :], prod[b % 2][:, :], ACT.Identity, bias=magic[:, :],
                                                 scale=fac[b % 2][:, 5:6]).then_inc(r8_ready, 1)
                        b = t
                        if b.within(0, B2):
                            act.wait_ge(g_ready, (b + 1).v)
                            nc.scalar.activation(relu[:, :], g_ps[b % 2][:, :], ACT.Relu).then_inc(relu_ready, 1)
                            act.wait_ge(relu_ready, (b + 1).v)
                            if b >= 1:
                                act.wait_ge(prod_ready, (b * 2).v)
                            nc.scalar.activation(relu2[:, :], relu[:, :], ACT.Square).then_inc(relu2_ready, 1)
                        b = t + 2
                        if b.within(0, B2):
                            act.wait_ge(x1_in[b % 2], ((b // 2) * 16 + 16).v)
                            if b >= 1:
                                act.wait_ge(tT_ready, b.v)
                            nc.scalar.activation(t8[:, :], row_of(b, 0, D), ACT.Identity, bias=row_of(b, OFFSET_COL, 1),
                                                 scale=row_of(b, SCALE_COL, 1)).then_inc(t8_ready, 1)

                    run_ticks(act, T2_FIRST, T2_LAST, T2_LOOP, T2_UNROLL, T2_TURNS, tick)

                @block.vector
                def _(dve):
                    chain = sem("chain2")
                    count = [0]

                    def link(ins):
                        count[0] += 1
                        ins.then_inc(chain, 1)
                        dve.wait_ge(chain, count[0])

                    sort_vector(dve, link, member2, E2, B1, B2, table1, table2, expert2, gather2, store2, 1)
                    dve.sem_inc(sorted2, 1)
                    link(dve.memset(magic[:, :], MAGIC))
                    means = w_mean[:, :].rearrange("p (e k) -> p k e", k=3)
                    link(dve.tensor_tensor(gu_mean[:, :], means[:, 0, :], means[:, 0, :], ALU.mult))
                    link(dve.tensor_tensor(gu_mean[:, :], gu_mean[:, :], means[:, 1, :], ALU.mult))
                    link(dve.memset(gu_block[:, :], 0.0))
                    link(dve.memset(d_block[:, :], 0.0))
                    for e in range(E2):
                        link(dve.tensor_scalar(is_expert[:, :], expert_f[:, 0:B2], float(e), None, ALU.is_equal))
                        dve.scalar_tensor_tensor(gu_block[:, :], is_expert[:, :], gu_mean[:, e:e + 1], gu_block[:, :],
                                                 ALU.mult, ALU.add)
                        link(dve.scalar_tensor_tensor(d_block[:, :], is_expert[:, :], w_mean[:, 3 * e + 2:3 * e + 3],
                                                      d_block[:, :], ALU.mult, ALU.add))

                    def tick(t):
                        b = t - 3
                        if b.within(0, B2):
                            dve.wait_ge(d_ready, (b + 1).v)
                            dve.wait_ge(factors, (b * 6 + 6).v)
                            dve.scalar_tensor_tensor(row_of(b, 0, D), d_ps[:, :], out_scale[:, bass.ds(b.v, 1)], row_of(b, 0, D),
                                                     ALU.mult, ALU.add).then_inc(out_ready, 1)
                        b = t + 1
                        if b.within(0, B2):
                            dve.wait_ge(tT_ready, (b + 1).v)
                            if b >= 1:
                                dve.wait_ge(u_ready, b.v)
                            dve.tensor_scalar(qT[:, :], tT_ps[:, :], MAGIC, MAGIC, ALU.add, ALU.subtract)\
                                .then_inc(qT_ready, 1)
                        b = t
                        if b.within(0, B2):
                            f = fac[b % 2]
                            dve.wait_ge(u_ready, (b + 1).v)
                            dve.wait_ge(relu2_ready, (b + 1).v)
                            if b >= 2:
                                dve.wait_ge(r8_ready, (b - 1).v)
                            dve.tensor_tensor(prod[b % 2][:, :], u_ps[b % 2][:, :], relu2[:, :], ALU.mult)\
                                .then_inc(prod_ready, 1)
                            dve.wait_ge(prod_ready, (b * 2 + 1).v)
                            dve.tensor_reduce(f[:, 0:1], prod[b % 2][:, :], X, ALU.max, apply_absolute_value=True)\
                                .then_inc(prod_ready, 1)
                            dve.tensor_scalar(f[:, 1:2], row_of(b, CUBE_COL, 1), gu_block[:, bass.ds(b.v, 1)], None,
                                              ALU.mult).then_inc(factors, 1)
                            dve.wait_ge(factors, (b * 6 + 1).v)
                            dve.wait_ge(prod_ready, (b * 2 + 2).v)
                            dve.tensor_scalar(f[:, 2:3], f[:, 0:1], f[:, 1:2], EPS, ALU.mult, ALU.max)\
                                .then_inc(factors, 1)
                            dve.wait_ge(factors, (b * 6 + 2).v)
                            dve.tensor_scalar(f[:, 3:4], f[:, 2:3], 1.0 / QMAX, None, ALU.mult).then_inc(factors, 1)
                            dve.wait_ge(factors, (b * 6 + 3).v)
                            dve.reciprocal(f[:, 4:5], f[:, 3:4]).then_inc(factors, 1)
                            dve.wait_ge(factors, (b * 6 + 4).v)
                            dve.tensor_scalar(out_scale[:, bass.ds(b.v, 1)], f[:, 3:4], d_block[:, bass.ds(b.v, 1)], None,
                                              ALU.mult).then_inc(factors, 1)
                            dve.tensor_scalar(f[:, 5:6], f[:, 1:2], f[:, 4:5], None, ALU.mult).then_inc(factors, 1)

                    run_ticks(dve, T2_FIRST, T2_LAST + 1, T2_LOOP, T2_UNROLL, T2_TURNS, tick)

                @block.tensor
                def _(pe):
                    sort_tensor(pe, member2, E2, B1, B2, 1)

                    def transpose(ps, src):
                        for k in range(K):
                            last = pe.transpose(ps[:, k * P:(k + 1) * P], src[:, k * P:(k + 1) * P], ident[:, :])
                        return last

                    def product(ps, left, e, kind):
                        for k in range(K):
                            last = pe.matmul(ps[:, :], left[:, k * P:(k + 1) * P],
                                             ternary[:, bass.ds(e * (3 * K * D) + (kind * K + k) * D, D)],
                                             start=(k == 0), stop=(k == K - 1))
                        return last

                    def tick(t):
                        b = t - 2
                        if b.within(0, B2):
                            pe.wait_ge(r8_ready, (b + 1).v)
                            if b >= 1:
                                pe.wait_ge(rT_ready, b.v)
                            transpose(rT_ps, r8).then_inc(rT_ps_ready, 1)
                        b = t
                        if b.within(0, B2):
                            e = pe.value_load(expert2[0:1, bass.ds(b.v, 1)], min_val=0, max_val=E2 - 1)
                            pe.wait_ge(qT_ready, (b + 1).v)
                            if b >= 2:
                                pe.wait_ge(prod_ready, (b * 2 - 3).v)
                            product(g_ps[b % 2], qT, e, 0).then_inc(g_ready, 1)
                            product(u_ps[b % 2], qT, e, 1).then_inc(u_ready, 1)
                        b = t + 1
                        if b.within(0, B2):
                            pe.wait_ge(t8_ready, (b + 1).v)
                            if b >= 1:
                                pe.wait_ge(qT_ready, b.v)
                            transpose(tT_ps, t8).then_inc(tT_ready, 1)
                        b = t - 2
                        if b.within(0, B2):
                            e = pe.value_load(expert2[0:1, bass.ds(b.v, 1)], min_val=0, max_val=E2 - 1)
                            pe.wait_ge(rT_ready, (b + 1).v)
                            if b >= 1:
                                pe.wait_ge(out_ready, b.v)
                            product(d_ps, rT, e, 2).then_inc(d_ready, 1)

                    pe.wait_ge(sorted2, 1)
                    run_ticks(pe, T2_FIRST, T2_LAST, T2_LOOP, T2_UNROLL, T2_TURNS, tick)

            stack.pop()


def kernel(x, itok_BxS_13_99985, ctx_2048, L0_ffn_router_w, L0_ffn_wg, L0_ffn_wu, L0_ffn_wd):
    import numpy as np
    import concourse.bacc as bacc
    from concourse.bass_utils import run_bass_kernel_spmd

    def chunked(w):
        n = w.shape[0]
        w = w.transpose(0, 2, 1).reshape(n, K, P, w.shape[1])
        return np.ascontiguousarray(w.transpose(0, 2, 1, 3).reshape(n, P, -1))

    wg, wu, wd = (np.asarray(w) for w in (L0_ffn_wg, L0_ffn_wu, L0_ffn_wd))
    arrays = {
        "x_rows": np.ascontiguousarray(np.asarray(x).reshape(N, D)),
        "token_ids_in": np.ascontiguousarray(np.asarray(itok_BxS_13_99985).reshape(TILES, P).T),
        "ctx_chunks": chunked(np.asarray(ctx_2048)),
        "router_chunks": chunked(np.asarray(L0_ffn_router_w)[None])[0],
        "weight_chunks": chunked(np.stack([wg, wu, wd], axis=1).reshape(MATS, D, D)),
    }
    nc = bacc.Bacc("TRN2", target_bir_lowering=False, num_devices=1, dynamic_dma_scratch_size=4096)
    args = [nc.dram_tensor(name, a.shape, mybir.dt.from_np(a.dtype), kind="ExternalInput").ap()
            for name, a in arrays.items()]
    out = nc.dram_tensor("out_rows", (N, D), F32, kind="ExternalOutput").ap()
    moe_program(nc, *args, out)
    r = run_bass_kernel_spmd(nc, [arrays], core_ids=[0])
    return np.asarray(r.results[0]["out_rows"]).reshape(np.asarray(x).shape)
```

```python
from contextlib import ExitStack

import concourse.bass as bass
from concourse import mybir

ALU = mybir.AluOpType
ACT = mybir.ActivationFunctionType
X = mybir.AxisListType.X
F32 = mybir.dt.float32
F32R = mybir.dt.float32r
BF16 = mybir.dt.bfloat16
F16 = mybir.dt.float16
I16 = mybir.dt.int16
I32 = mybir.dt.int32
U32 = mybir.dt.uint32

P = 128
N = 2048
D = 512
K = D // P
TILES = N // P
E1, E2 = 4, 8
B1 = TILES + E1 - 1
B2 = TILES + E2 - 1
MATS = 3 * E2
ID_STEP = 25000 // E1
EPS = 1e-5
QMAX = 127.0
MAGIC = 12582912.0
ROW = D + 4
SCALE_COL, OFFSET_COL, STEP_COL, CUBE_COL = range(D, D + 4)
EARLY = 1
MADE = 10
DVE_COLS = 1024
RING = 4
HOT_CHUNK = 4


class At:

    def __init__(self, first, stride=0, turn=None):
        self.first, self.stride, self.turn = first, stride, turn

    def __add__(self, n):
        return At(self.first + n, self.stride, self.turn)

    def __sub__(self, n):
        return self + -n

    def __mul__(self, n):
        return At(self.first * n, self.stride * n, self.turn)

    def __floordiv__(self, n):
        assert self.stride % n == 0
        return At(self.first // n, self.stride // n, self.turn)

    def __mod__(self, n):
        assert self.stride % n == 0
        return self.first % n

    def __ge__(self, n):
        return self.first >= n

    @property
    def v(self):
        return self.first if self.turn is None else self.turn * self.stride + self.first

    def within(self, low, high, turns=1):
        if self.turn is not None:
            assert low <= self.first, (low, self.first)
            return True
        return low <= self.first < high


def run_ticks(eng, first, last, loop_first, unroll, turns, tick):
    for t in range(first, loop_first):
        tick(At(t))
    with eng.Fori(0, turns) as turn:
        for u in range(unroll):
            tick(At(loop_first + u, unroll, turn))
    for t in range(loop_first + unroll * turns, last + 1):
        tick(At(t))


T1_FIRST, T1_LAST, T1_LOOP, T1_UNROLL, T1_TURNS = -2, B1 + 2, 5, 4, 3
T2_FIRST, T2_LAST, T2_LOOP, T2_UNROLL, T2_TURNS = -2, B2 + 2, 4, 4, 4
assert T1_LOOP + T1_UNROLL * T1_TURNS + 1 <= B1
assert T2_LOOP + T2_UNROLL * T2_TURNS + 2 <= B2


def moe_program(nc, x_in, tokens_in, ctx_in, router_in, weights_in, out):
    with ExitStack() as whole:
        stack = [whole]

        def sb(name, shape, dt):
            return stack[-1].enter_context(nc.sbuf_tensor(name, shape, dt))

        def sem(name):
            return whole.enter_context(nc.semaphore(name))

        x1_rows = nc.dram_tensor("x1_rows", [N, ROW], F32).ap()

        bank = [whole.enter_context(nc.psum_tensor(f"bank{i}", [P, D], F32)) for i in range(8)]

        ternary = sb("ternary", [P, MATS * K * D], BF16)
        ident = sb("ident", [P, P], F32)
        before = sb("before", [P, P], F32)
        ones = sb("ones", [P, P], F32)
        iota_i = sb("iota_i", [P, P], I32)
        iota = sb("iota", [P, P], F32)
        iota16 = sb("iota16", [P, P], F16)
        half_powers = sb("half_powers", [P, 2], F32)
        token1 = sb("token1", [P, TILES], F32)
        token1_i = sb("token1_i", [P, TILES], I32)
        token_ids = sb("token_ids", [P, TILES], I32)
        at_least = sb("at_least", [P, (E1 + 1) * TILES], F32)
        member1 = sb("member1", [P, E1 * TILES], F32)
        member2 = sb("member2", [P, E2 * B1], F32)
        scan = sb("scan", [P, max(E2 * B1, (E2 - 1) * B2)], F32)
        earlier = sb("earlier", [P, E2 * B1], F32)
        placed = sb("placed", [P, E2 * B1], F32)
        place = sb("place", [P, B1], F32)
        place_block = sb("place_block", [P, B1], F32)
        place_row = sb("place_row", [P, B1], F32)
        small = sb("small", [P, 10, E2], F32)
        table1 = sb("table1", [P, B1], F32)
        valid1 = sb("valid1", [P, B1], F32)
        choice = sb("choice", [P, B1], F32)
        pad = sb("pad", [P, B2], F32)
        gather1 = sb("gather1", [P, B1], I32)
        store1 = sb("store1", [P, B1], I32)
        gather2 = sb("gather2", [P, B2], I32)
        store2 = sb("store2", [P, B2], I32)
        expert_f = sb("expert_f", [P, B2], F32)
        expert1 = sb("expert1", [P, B1], I32)
        expert2 = sb("expert2", [P, B2], I32)
        router = sb("router", [P, K * E2], F32)
        router_sum = sb("router_sum", [P, E2], F32)
        abs_sum = sb("abs_sum", [P, MATS], F32)
        w_mean = sb("w_mean", [P, MATS], F32)
        w_scale = sb("w_scale", [P, MATS], F32)

        inputs_in = sem("inputs_in")
        made = sem("made")
        pool_passed, dve_passed, pe_passed = sem("pool_passed"), sem("dve_passed"), sem("pe_passed")
        sorting = sem("sorting")
        sort_pe = sem("sort_pe")
        placing, hot_ready = sem("placing"), sem("hot_ready")
        sorted1, sorted2 = sem("sorted1"), sem("sorted2")
        sorted_sem = (sorted1, sorted2)

        def sort_vector(dve, link, member, n_exp, n_tiles, n_blocks, tokens, experts, gather, store, hots, lap,
                        meanwhile):
            width = n_exp * n_tiles
            m = member[:, 0:width]
            m3 = m.rearrange("p (e t) -> p e t", e=n_exp)
            blocks, blocks_sum, excess, excess_sum, start, lift, part = (small[:, i, 0:n_exp] for i in range(7))
            count_ps = bank[7][:, 256:256 + n_exp]
            dve.tensor_reduce(part, m3, X, ALU.add)
            link(dve.tensor_tensor_scan(scan[:, 0:width], ones_wide[:, 0:width], m, 0.0, ALU.mult, ALU.add))
            link(dve.tensor_tensor(earlier[:, 0:width], scan[:, 0:width], m, ALU.subtract))
            dve.sem_inc(sorting, 1)
            meanwhile()
            dve.wait_ge(sort_pe, 2 * lap + 1)
            link(dve.tensor_scalar(blocks, count_ps, 1.0 / P, 0.5 - 0.5 / P, ALU.mult, ALU.add))
            link(dve.tensor_scalar(blocks, blocks, MAGIC, MAGIC, ALU.add, ALU.subtract))
            link(dve.scalar_tensor_tensor(excess, blocks, float(P), count_ps, ALU.mult, ALU.subtract))
            dve.tensor_tensor_scan(blocks_sum, ones[:, 0:n_exp], blocks, 0.0, ALU.mult, ALU.add)
            link(dve.tensor_tensor_scan(excess_sum, ones[:, 0:n_exp], excess, 0.0, ALU.mult, ALU.add))
            dve.tensor_tensor(start, blocks_sum, blocks, ALU.subtract)
            link(dve.tensor_tensor(lift, excess_sum, excess, ALU.subtract))
            wide = [P, n_exp, n_tiles]
            rank3 = bank[7][:, 0:width].rearrange("p (e t) -> p e t", e=n_exp)
            placed3 = placed[:, 0:width].rearrange("p (e t) -> p e t", e=n_exp)
            link(dve.tensor_tensor(placed3, rank3, small[:, 5, 0:n_exp, None].to_broadcast(wide), ALU.add))
            link(dve.tensor_tensor(placed3, placed3, m3, ALU.mult))
            link(dve.tensor_reduce(place[:, 0:n_tiles], placed[:, 0:width].rearrange("p (e t) -> p t e", e=n_exp),
                                   X, ALU.add))
            link(dve.tensor_scalar(place_block[:, 0:n_tiles], place[:, 0:n_tiles], 1.0 / P, 0.5 / P - 0.5,
                                   ALU.mult, ALU.add))
            link(dve.tensor_scalar(place_block[:, 0:n_tiles], place_block[:, 0:n_tiles], MAGIC, MAGIC,
                                   ALU.add, ALU.subtract))
            dve.scalar_tensor_tensor(place_row[:, 0:n_tiles], place_block[:, 0:n_tiles], -float(P),
                                     place[:, 0:n_tiles], ALU.mult, ALU.add).then_inc(placing, 1)
            row_hot, block_hot = hots
            wide = [P, n_tiles, n_blocks]
            link(dve.tensor_tensor(block_hot[:, :, 0:n_blocks], iota[:, None, 0:n_blocks].to_broadcast(wide),
                                   place_block[:, 0:n_tiles, None].to_broadcast(wide), ALU.is_equal))
            dve.tensor_tensor(block_hot[:, :, 0:n_blocks], block_hot[:, :, 0:n_blocks],
                              tokens[:, 0:n_tiles, None].to_broadcast(wide), ALU.mult)
            dve.wait_ge(placing, lap + 1)
            for t in range(n_tiles):
                hot = dve.tensor_scalar(row_hot[:, t, :], iota16[:, :], place_row[:, t:t + 1], None, ALU.is_equal)
                if t % HOT_CHUNK == HOT_CHUNK - 1 or t == n_tiles - 1:
                    hot.then_inc(hot_ready, 1)
            wide = [P, n_blocks, n_exp - 1]
            started = scan[:, 0:n_blocks * (n_exp - 1)].rearrange("p (b e) -> p b e", b=n_blocks)
            link(dve.tensor_tensor(started, iota[:, 0:n_blocks, None].to_broadcast(wide),
                                   small[:, 4:5, 1:n_exp].to_broadcast(wide), ALU.is_ge))
            link(dve.tensor_reduce(expert_f[:, 0:n_blocks], started, X, ALU.add))
            link(dve.tensor_copy(experts[:, 0:n_blocks], expert_f[:, 0:n_blocks]))
            table_ps = bank[6][:, 0:n_blocks]
            dve.wait_ge(sort_pe, 2 * lap + 2)
            link(dve.tensor_scalar(pad[:, 0:n_blocks], table_ps, 0.0, None, ALU.is_equal))
            link(dve.scalar_tensor_tensor(gather[:, 0:n_blocks], table_ps, -1.0, pad[:, 0:n_blocks],
                                          ALU.add, ALU.add))
            dve.sem_inc(sorted_sem[lap], 1)
            link(dve.scalar_tensor_tensor(pad[:, 0:n_blocks], pad[:, 0:n_blocks], float(2 * N), table_ps,
                                          ALU.mult, ALU.add))
            link(dve.tensor_scalar(store[:, 0:n_blocks], pad[:, 0:n_blocks], -1.0, None, ALU.add))

        def sort_tensor(pe, member, n_exp, n_tiles, n_blocks, hots, chunks_before, lap):
            width = n_exp * n_tiles
            pe.wait_ge(sorting, lap + 1)
            pe.matmul(bank[7][:, 0:width], before[:, :], member[:, 0:width], start=True, stop=False)
            pe.matmul(bank[7][:, 0:width], ones[:, 0:P], earlier[:, 0:width], start=False, stop=True)
            pe.matmul(bank[7][:, 256:256 + n_exp], ones[:, 0:P], small[:, 6, 0:n_exp], start=True,
                      stop=True).then_inc(sort_pe, 1)
            row_hot, block_hot = hots
            for t in range(n_tiles):
                if t % HOT_CHUNK == 0:
                    pe.wait_ge(hot_ready, chunks_before + t // HOT_CHUNK + 1)
                last = pe.matmul(bank[6][:, 0:n_blocks], row_hot[:, t, :], block_hot[:, t, 0:n_blocks],
                                 start=(t == 0), stop=(t == n_tiles - 1))
            last.then_inc(sort_pe, 1)

        ones_wide = sb("ones_wide", [P, E2 * B1], F32)

        with ExitStack() as inner:
            stack.append(inner)
            ctx_hi = sb("ctx_hi", [P, E1 * K * D], F32R)
            ctx_lo = sb("ctx_lo", [P, E1 * K * D], F32R)
            staged = [sb(f"staged{i}", [P, K * D], F32) for i in range(2)]
            x = [sb(f"x{i}", [P, D], F32) for i in range(RING)]
            h = sb("h", [P, D], F32)
            hT_hi = sb("hT_hi", [P, D], F32R)
            hT_lo = sb("hT_lo", [P, D], F32R)
            sil = sb("sil", [P, D], F32)
            p = sb("p", [P, D], F32)
            pT_hi = sb("pT_hi", [P, D], F32R)
            pT_lo = sb("pT_lo", [P, D], F32R)
            row = [sb(f"row{i}", [P, ROW], F32) for i in range(2)]
            squares = sb("squares", [P, D], F32)
            x1T = sb("x1T", [P, D], F32)
            stats1 = sb("stats1", [P, 6], F32)
            mv1 = [sb(f"mv1_{i}", [P, 2], F32) for i in range(2)]
            ln1 = [sb(f"ln1_{i}", [P, 3], F32) for i in range(2)]
            ln2 = [sb(f"ln2_{i}", [P, 9], F32) for i in range(2)]
            best = sb("best", [P, 8], F32)
            best_at = sb("best_at", [P, 8], U32)
            gather_at = [sb(f"gather_at{i}", [P, 1], I32) for i in range(RING)]
            store_at = [sb(f"store_at{i}", [P, 1], I32) for i in range(2)]

            def spare(matrix, n, dt):
                first = matrix * K * D
                return ternary[:, first:first + n].bitcast(dt)

            hots1 = (spare(12, TILES * P, F16).rearrange("p (t r) -> p t r", t=TILES),
                     spare(13, TILES * B2, F16).rearrange("p (t b) -> p t b", t=TILES))
            ctx_raw = [spare(16 + 2 * e, 2 * K * D, F32) for e in range(E1)]

            ctx_in_sem = [sem(f"ctx_in{e}") for e in range(E1)]
            staged_in = [sem(f"staged_in{i}") for i in range(2)]
            ctx_hi_ready, ctx_lo_ready = sem("ctx_hi_ready"), sem("ctx_lo_ready")
            table_read = sem("table_read")
            gather_at_ready, store_at_ready = sem("gather_at_ready"), sem("store_at_ready")
            x_in_sem = [sem(f"x_in{i}") for i in range(RING)]
            moments1 = sem("moments1")
            norm1 = sem("norm1")
            h_ready, hT_ready, hT_hi_ready, hT_lo_ready = (sem(n) for n in ("h_ready", "hT_ready", "hT_hi_ready", "hT_lo_ready"))
            a_ready, sil_ready, p_ready = (sem(n) for n in ("a_ready", "sil_ready", "p_ready"))
            pT_ready, pT_hi_ready, pT_lo_ready = (sem(n) for n in ("pT_ready", "pT_hi_ready", "pT_lo_ready"))
            y_ready, x1_ready, mean2_ready, norm2 = (sem(n) for n in ("y_ready", "x1_ready", "mean2_ready", "norm2"))
            squares_ready, x1T_ready, x1T_copied, logits_ready = (sem(n) for n in ("squares_ready", "x1T_ready", "x1T_copied", "logits_ready"))
            largest_ready, step_ready, step_inv, quant_ready = (sem(n) for n in ("largest_ready", "step_ready", "step_inv", "quant_ready"))
            routed, chosen = sem("routed"), sem("chosen")
            router_sum_ready, router_mean_ready, centred = (
                sem(n) for n in ("router_sum_ready", "router_mean_ready", "centred"))
            row_out = [sem(f"row_out{i}") for i in range(2)]
            abs_ready, mean_ready, tern, tern_act = (sem(n) for n in ("abs_ready", "mean_ready", "tern", "tern_act"))

            hT_ps, pT_ps, x1T_ps, y_ps = bank[0], bank[1], bank[2], bank[3]
            a_ps = [bank[4], bank[5]]
            mean_ps, logits_ps = bank[6], bank[7]

            with nc.Block() as block:

                @block.sync
                def _(sp):
                    sp.dma_start(token_ids[:, :], tokens_in).then_inc(inputs_in, 16)
                    sp.dma_start(router[:, :], router_in).then_inc(inputs_in, 16)
                    for e in range(E1):
                        sp.dma_start(ctx_raw[e], ctx_in[e]).then_inc(ctx_in_sem[e], 16)

                    def load(m):
                        if m >= 2:
                            sp.wait_ge(tern, (m * 4 - 5).v)
                            sp.wait_ge(tern_act, (m - 1).v)
                        sp.dma_start(staged[m % 2][:, :], weights_in[bass.ds(m.v, 1)].rearrange("a p n -> (a p) n"))\
                          .then_inc(staged_in[m % 2], 16)

                    for m in range(2):
                        load(At(m))
                    with sp.Fori(0, MATS // 2 - 1) as turn:
                        for u in range(2):
                            load(At(2 + u, 2, turn))

                @block.gpsimd
                def _(pool):
                    pool.iota(iota_i[:, :], [[1, P]], base=0, channel_multiplier=0).then_inc(made, 1)
                    pool.iota(token1_i[:, :], [[P, TILES]], base=1, channel_multiplier=1).then_inc(made, 1)
                    pool.memset(ones[:, :], 1.0).then_inc(made, 1)
                    pool.memset(ones_wide[:, :], 1.0).then_inc(made, 1)
                    pool.memset(before[:, :], 0.0).then_inc(made, 1)
                    pool.memset(ident[:, :], 0.0).then_inc(made, 1)
                    pool.memset(half_powers[:, 0:1], -0.5).then_inc(made, 1)
                    pool.memset(half_powers[:, 1:2], 0.5).then_inc(made, 1)
                    pool.wait_ge(made, 8)
                    pool.affine_select(before[:, :], before[:, :], [[-1, P]], ALU.is_ge, 1.0, base=0,
                                       channel_multiplier=1).then_inc(made, 1)
                    pool.affine_select(ident[:, :], ident[:, :], [[-1, P]], ALU.not_equal, 1.0, base=0,
                                       channel_multiplier=1).then_inc(made, 1)

                    def tick(t):
                        b = t + 1
                        if b.within(0, B1):
                            s = ln1[b % 2]
                            if b >= 2:
                                pool.wait_ge(h_ready, (b - 1).v)
                            pool.wait_ge(moments1, (b * 2 + 2).v)
                            pool.sem_inc(pool_passed, 1)
                            pool.tensor_scalar(s[:, 0:1], mv1[b % 2][:, 1:2], EPS, None, ALU.add).then_inc(norm1, 1)
                            pool.wait_ge(norm1, (b * 3 + 1).v)
                            pool.sem_inc(pool_passed, 1)
                            pool.tensor_tensor(s[:, 1:2], s[:, 0:1], half_powers[:, 0:1], ALU.pow).then_inc(norm1, 1)
                            pool.wait_ge(norm1, (b * 3 + 2).v)
                            pool.sem_inc(pool_passed, 1)
                            pool.tensor_scalar(s[:, 2:3], mv1[b % 2][:, 0:1], s[:, 1:2], -1.0, ALU.mult, ALU.mult)\
                                .then_inc(norm1, 1)
                        b = t - 3
                        if b.within(0, B1):
                            s, r = ln2[b % 2], row[b % 2]
                            pool.wait_ge(step_inv, (b + 1).v)
                            pool.sem_inc(pool_passed, 1)
                            pool.tensor_scalar(r[:, SCALE_COL:SCALE_COL + 1], s[:, 5:6], s[:, 8:9], None, ALU.mult)\
                                .then_inc(quant_ready, 1)
                            st = r[:, STEP_COL:STEP_COL + 1]
                            pool.tensor_scalar(r[:, CUBE_COL:CUBE_COL + 1], st, st, st, ALU.mult, ALU.mult)\
                                .then_inc(quant_ready, 1)
                            pool.wait_ge(quant_ready, (b * 3 + 1).v)
                            pool.sem_inc(pool_passed, 1)
                            pool.tensor_scalar(r[:, OFFSET_COL:OFFSET_COL + 1], r[:, SCALE_COL:SCALE_COL + 1],
                                               s[:, 1:2], None, ALU.mult).then_inc(quant_ready, 1)
                        b = t + 2
                        if b.within(0, B1):
                            if b >= RING:
                                pool.wait_ge(x1_ready, (b - (RING - 1)).v)
                                pool.sem_inc(pool_passed, 1)
                            pool.tensor_copy(gather_at[b % RING][:, :], gather1[:, bass.ds(b.v, 1)])\
                                .then_inc(gather_at_ready, 1)
                            pool.wait_ge(gather_at_ready, (b + 1).v)
                            pool.sem_inc(pool_passed, 1)
                            pool.indirect_dma_start(x[b % RING][:, :], None, x_in,
                                                    bass.IndirectOffsetOnAxis(ap=gather_at[b % RING][:, :], axis=0),
                                                    bounds_check=N - 1, oob_is_err=False)\
                                .then_inc(x_in_sem[b % RING], 16)
                        b = t - 3
                        if b.within(0, B1):
                            r = row[b % 2]
                            if b >= 2:
                                pool.wait_ge(row_out[b % 2], ((b // 2) * 16).v)
                                pool.sem_inc(pool_passed, 1)
                            pool.tensor_copy(store_at[b % 2][:, :], store1[:, bass.ds(b.v, 1)])\
                                .then_inc(store_at_ready, 1)
                            pool.wait_ge(store_at_ready, (b + 1).v)
                            pool.wait_ge(quant_ready, (b * 3 + 3).v)
                            pool.sem_inc(pool_passed, 1)
                            pool.indirect_dma_start(x1_rows, bass.IndirectOffsetOnAxis(ap=store_at[b % 2][:, :], axis=0),
                                                    r[:, :], None, bounds_check=N - 1, oob_is_err=False)\
                                .then_inc(row_out[b % 2], 16)
                        b = t - 3
                        if b.within(0, B1):
                            pool.wait_ge(routed, (b * 2 + 2).v)
                            pool.sem_inc(pool_passed, 1)
                            pool.tensor_copy(choice[:, bass.ds(b.v, 1)], best_at[:, 0:1]).then_inc(chosen, 1)
                        b = t - 2
                        if b.within(0, B1):
                            s = ln2[b % 2]
                            pool.wait_ge(squares_ready, (b + 1).v)
                            pool.sem_inc(pool_passed, 1)
                            pool.tensor_scalar(s[:, 3:4], s[:, 2:3], 1.0 / D, EPS, ALU.mult, ALU.add).then_inc(norm2, 1)
                            pool.wait_ge(norm2, (b * 2 + 1).v)
                            pool.wait_ge(largest_ready, (b + 1).v)
                            pool.sem_inc(pool_passed, 1)
                            pool.tensor_tensor(s[:, 5:7], s[:, 3:5], half_powers[:, :], ALU.pow).then_inc(norm2, 1)
                            pool.wait_ge(norm2, (b * 2 + 2).v)
                            pool.sem_inc(pool_passed, 1)
                            pool.tensor_scalar(s[:, 7:8], s[:, 6:7], s[:, 5:6], None, ALU.mult).then_inc(step_ready, 1)
                            pool.wait_ge(step_ready, (b * 2 + 1).v)
                            pool.sem_inc(pool_passed, 1)
                            pool.tensor_scalar(row[b % 2][:, STEP_COL:STEP_COL + 1], s[:, 7:8], EPS, 1.0 / QMAX,
                                               ALU.max, ALU.mult).then_inc(step_ready, 1)

                    pool.wait_ge(sorted1, 1)
                    run_ticks(pool, T1_FIRST, T1_LAST, T1_LOOP, T1_UNROLL, T1_TURNS, tick)
                    for i in range(2):
                        pool.wait_ge(row_out[i], 16 * ((B1 - i + 1) // 2))

                @block.scalar
                def _(act):
                    act.preload_act_table(ACT.Silu)
                    for e in range(E1):
                        act.wait_ge(ctx_in_sem[e], 16)
                        nc.scalar.activation(ctx_hi[:, e * K * D:(e + 1) * K * D], ctx_raw[e], ACT.Copy)\
                            .then_inc(ctx_hi_ready, 1)

                    def sum_abs(m):
                        act.wait_ge(staged_in[m % 2], ((m // 2) * 16 + 16).v)
                        nc.scalar.activation(ternary[:, bass.ds((m * (K * D)).v, K * D)], staged[m % 2][:, :], ACT.Abs,
                                             accum_out=abs_sum[:, bass.ds(m.v, 1)]).then_inc(abs_ready, 1)

                    def scale_part(m):
                        act.wait_ge(tern, (m * 4 + 2).v)
                        nc.scalar.activation(
                            ternary[:, bass.ds((m * (K * D) + DVE_COLS).v, K * D - DVE_COLS)].bitcast(I16),
                            staged[m % 2][:, DVE_COLS:], ACT.Copy, scale=w_scale[:, bass.ds(m.v, 1)])\
                            .then_inc(tern_act, 1)

                    def tick(t):
                        b = t - 1
                        if b.within(0, B1):
                            act.wait_ge(pT_ready, (b + 1).v)
                            nc.scalar.activation(pT_hi[:, :], pT_ps[:, :], ACT.Copy).then_inc(pT_hi_ready, 1)
                        b = t - 2
                        if b.within(0, B1):
                            act.wait_ge(mean2_ready, (b + 1).v)
                            if b >= 1:
                                act.wait_ge(largest_ready, b.v)
                            s = ln2[b % 2]
                            nc.scalar.activation(squares[:, :], row[b % 2][:, 0:D], ACT.Square, bias=s[:, 1:2],
                                                 accum_out=s[:, 2:3]).then_inc(squares_ready, 1)
                        b = t + 1
                        if b.within(0, B1):
                            act.wait_ge(norm1, (b * 3 + 3).v)
                            if b >= 1:
                                act.wait_ge(hT_ready, b.v)
                            s = ln1[b % 2]
                            nc.scalar.activation(h[:, :], x[b % RING][:, :], ACT.Identity, bias=s[:, 2:3],
                                                 scale=s[:, 1:2]).then_inc(h_ready, 1)
                        b = t
                        if b.within(0, B1):
                            act.wait_ge(a_ready, (b + 1).v)
                            if b >= 1:
                                act.wait_ge(p_ready, b.v)
                            nc.scalar.activation(sil[:, :], a_ps[b % 2][:, :], ACT.Silu).then_inc(sil_ready, 1)
                        b = t - 2
                        if b.within(0, B1):
                            act.wait_ge(x1T_ready, (b + 1).v)
                            if b >= 1:
                                act.wait_ge(logits_ready, b.v)
                            nc.scalar.activation(x1T[:, :], x1T_ps[:, :], ACT.Copy).then_inc(x1T_copied, 1)
                        b = t + 1
                        if b.within(0, B1):
                            act.wait_ge(hT_ready, (b + 1).v)
                            if b >= 1:
                                act.wait_ge(a_ready, b.v)
                            nc.scalar.activation(hT_hi[:, :], hT_ps[:, :], ACT.Copy).then_inc(hT_hi_ready, 1)
                        m = t + (1 + EARLY)
                        if m.within(EARLY - 1, MATS):
                            scale_part(m)
                        m = t + (2 + EARLY)
                        if m.within(EARLY, MATS):
                            sum_abs(m)

                    for m in range(EARLY):
                        sum_abs(At(m))
                        if m >= 1:
                            scale_part(At(m - 1))
                    run_ticks(act, T1_FIRST, T1_LAST, T1_LOOP, T1_UNROLL, T1_TURNS, tick)

                @block.vector
                def _(dve):
                    chain = sem("chain1")
                    count = [0]

                    def link(ins):
                        count[0] += 1
                        ins.then_inc(chain, 1)
                        dve.wait_ge(chain, count[0])

                    dve.wait_ge(made, MADE)
                    dve.wait_ge(inputs_in, 32)
                    dve.tensor_copy(iota[:, :], iota_i[:, :])
                    dve.tensor_copy(iota16[:, :], iota_i[:, :])
                    link(dve.tensor_copy(token1[:, :], token1_i[:, :]))
                    dve.memset(at_least[:, 0:TILES], 1.0)
                    dve.memset(at_least[:, E1 * TILES:], 0.0)
                    for e in range(1, E1):
                        last = dve.tensor_scalar(at_least[:, e * TILES:(e + 1) * TILES], token_ids[:, :],
                                                 float(e * ID_STEP), None, ALU.is_ge)
                    link(last)
                    link(dve.tensor_tensor(member1[:, :], at_least[:, 0:E1 * TILES], at_least[:, TILES:], ALU.subtract))
                    def centre_router():
                        router3 = router[:, :].rearrange("p (k e) -> p k e", k=K)
                        dve.wait_ge(router_mean_ready, 1)
                        link(dve.tensor_scalar(router_sum[:, :], logits_ps[:, 0:E2], 1.0 / D, None, ALU.mult))
                        dve.tensor_tensor(router3, router3, router_sum[:, None, :].to_broadcast([P, K, E2]),
                                          ALU.subtract).then_inc(centred, 1)

                    dve.tensor_reduce(router_sum[:, :], router[:, :].rearrange("p (k e) -> p e k", k=K), X,
                                      ALU.add).then_inc(router_sum_ready, 1)
                    sort_vector(dve, link, member1, E1, TILES, B1, token1, expert1, gather1, store1, hots1, 0,
                                centre_router)
                    link(dve.tensor_copy(table1[:, :], bank[6][:, 0:B1]))
                    dve.sem_inc(table_read, 1)
                    link(dve.tensor_scalar(valid1[:, :], table1[:, :], 0.0, None, ALU.is_gt))
                    def low_halves(e):
                        cols = slice(e * K * D, (e + 1) * K * D)
                        dve.wait_ge(ctx_hi_ready, e + 1)
                        dve.tensor_tensor(ctx_lo[:, cols], ctx_raw[e], ctx_hi[:, cols].bitcast(F32),
                                          ALU.subtract).then_inc(ctx_lo_ready, 1)

                    def mean_of(m):
                        one = bass.ds(m.v, 1)
                        dve.wait_ge(mean_ready, (m + 1).v)
                        dve.tensor_scalar(w_mean[:, one], mean_ps[:, bass.ds((m + 64).v, 1)], 1.0 / (D * D), EPS,
                                          ALU.mult, ALU.max).then_inc(tern, 1)

                    def scale_of(m):
                        one = bass.ds(m.v, 1)
                        dve.wait_ge(tern, (m * 4 + 1).v)
                        dve.reciprocal(w_scale[:, one], w_mean[:, one]).then_inc(tern, 1)

                    def scale_part(m):
                        one = bass.ds(m.v, 1)
                        dve.wait_ge(tern, (m * 4 + 2).v)
                        dve.tensor_scalar(ternary[:, bass.ds((m * (K * D)).v, DVE_COLS)].bitcast(I16),
                                          staged[m % 2][:, 0:DVE_COLS], w_scale[:, one], None,
                                          ALU.mult).then_inc(tern, 1)

                    def cut(m):
                        cols = bass.ds((m * (K * D)).v, K * D)
                        dve.wait_ge(tern, (m * 4 + 3).v)
                        dve.wait_ge(tern_act, (m + 1).v)
                        dve.tensor_scalar(ternary[:, cols], ternary[:, cols].bitcast(I16), 1.0, -1.0,
                                          ALU.min, ALU.max).then_inc(tern, 1)

                    def tick(t):
                        b = t - 2
                        if b.within(0, B1):
                            dve.wait_ge(y_ready, (b + 1).v)
                            if b >= 2:
                                dve.wait_ge(row_out[b % 2], ((b // 2) * 16).v)
                            dve.scalar_tensor_tensor(row[b % 2][:, 0:D], y_ps[:, :], 1.0, x[b % RING][:, :], ALU.mult,
                                                     ALU.add, accum_out=ln2[b % 2][:, 0:1]).then_inc(x1_ready, 1)
                        b = t - 3
                        if b.within(0, B1):
                            dve.wait_ge(logits_ready, (b + 1).v)
                            dve.sem_inc(dve_passed, 1)
                            dve.max(best[:, :], logits_ps[:, 0:E2]).then_inc(routed, 1)
                        b = t - 2
                        if b.within(0, B1):
                            dve.wait_ge(x1_ready, (b + 1).v)
                            dve.tensor_scalar(ln2[b % 2][:, 1:2], ln2[b % 2][:, 0:1], -1.0 / D, None, ALU.mult)\
                                .then_inc(mean2_ready, 1)
                        m = t + EARLY
                        if m.within(EARLY - 1, MATS):
                            cut(m)
                        b = t - 3
                        if b.within(0, B1):
                            dve.wait_ge(routed, (b * 2 + 1).v)
                            if b >= 1:
                                dve.wait_ge(chosen, b.v)
                            dve.sem_inc(dve_passed, 1)
                            dve.max_index(best_at[:, :], best[:, :], logits_ps[:, 0:E2]).then_inc(routed, 1)
                        b = t - 1
                        if b.within(0, B1):
                            dve.wait_ge(pT_hi_ready, (b + 1).v)
                            if b >= 1:
                                dve.wait_ge(y_ready, b.v)
                            dve.tensor_tensor(pT_lo[:, :], pT_ps[:, :], pT_hi[:, :].bitcast(F32), ALU.subtract)\
                                .then_inc(pT_lo_ready, 1)
                        b = t - 2
                        if b.within(0, B1):
                            dve.wait_ge(squares_ready, (b + 1).v)
                            dve.tensor_reduce(ln2[b % 2][:, 4:5], squares[:, :], X, ALU.max).then_inc(largest_ready, 1)
                        m = t + (1 + EARLY)
                        if m.within(EARLY - 1, MATS):
                            mean_of(m)
                        m = t + (1 + EARLY)
                        if m.within(EARLY - 1, MATS):
                            scale_of(m)
                        b = t
                        if b.within(0, B1):
                            dve.wait_ge(sil_ready, (b + 1).v)
                            if b >= 1:
                                dve.wait_ge(pT_ready, b.v)
                            dve.tensor_tensor(p[:, :], a_ps[b % 2][:, :], sil[:, :], ALU.mult).then_inc(p_ready, 1)
                        b = t + 1
                        if b.within(0, B1):
                            dve.wait_ge(hT_hi_ready, (b + 1).v)
                            dve.tensor_tensor(hT_lo[:, :], hT_ps[:, :], hT_hi[:, :].bitcast(F32), ALU.subtract)\
                                .then_inc(hT_lo_ready, 1)
                        b = t + 2
                        if b.within(0, B1):
                            dve.wait_ge(x_in_sem[b % RING], ((b // RING) * 16 + 16).v)
                            dve.bn_stats(stats1[:, :], x[b % RING][:, :]).then_inc(moments1, 1)
                        m = t + (1 + EARLY)
                        if m.within(EARLY - 1, MATS):
                            scale_part(m)
                        b = t + 2
                        if b.within(0, B1):
                            dve.wait_ge(moments1, (b * 2 + 1).v)
                            if b >= 2:
                                dve.wait_ge(norm1, (b * 3 - 3).v)
                            dve.sem_inc(dve_passed, 1)
                            dve.bn_aggr(mv1[b % 2][:, :], stats1[:, :]).then_inc(moments1, 1)
                        b = t - 2
                        if b.within(0, B1):
                            dve.wait_ge(step_ready, (b * 2 + 2).v)
                            dve.reciprocal(ln2[b % 2][:, 8:9], row[b % 2][:, STEP_COL:STEP_COL + 1]).then_inc(step_inv, 1)

                    low_halves(0)
                    tick(At(T1_FIRST))
                    low_halves(1)
                    tick(At(T1_FIRST + 1))
                    low_halves(2)
                    low_halves(3)
                    run_ticks(dve, T1_FIRST + 2, T1_LAST, T1_LOOP, T1_UNROLL, T1_TURNS, tick)

                @block.tensor
                def _(pe):
                    pe.wait_ge(made, MADE)
                    pe.wait_ge(router_sum_ready, 1)
                    pe.matmul(logits_ps[:, 0:E2], ones[:, 0:P], router_sum[:, :], start=True,
                              stop=True).then_inc(router_mean_ready, 1)
                    pe.wait_ge(centred, 1)
                    sort_tensor(pe, member1, E1, TILES, B1, hots1, 0, 0)

                    def sum_mean(m):
                        pe.wait_ge(abs_ready, (m + 1).v)
                        if m >= 1:
                            pe.wait_ge(tern, (m * 4 - 3).v)
                        else:
                            pe.wait_ge(table_read, 1)
                        pe.matmul(mean_ps[:, bass.ds((m + 64).v, 1)], ones[:, 0:P], abs_sum[:, bass.ds(m.v, 1)],
                                  start=True, stop=True).then_inc(mean_ready, 1)

                    def transpose(ps, src):
                        for k in range(K):
                            last = pe.transpose(ps[:, k * P:(k + 1) * P], src[:, k * P:(k + 1) * P], ident[:, :])
                        return last

                    def expert_of(b):
                        return pe.value_load(expert1[0:1, bass.ds(b.v, 1)], min_val=0, max_val=E1 - 1)

                    def product(ps, hi, lo, e):
                        pairs = [(hi, ctx_hi), (hi, ctx_lo), (lo, ctx_hi)]
                        for n, (left, right) in enumerate(pairs):
                            for k in range(K):
                                last = pe.matmul(ps[:, :], left[:, k * P:(k + 1) * P],
                                                 right[:, bass.ds(e * (K * D) + k * D, D)],
                                                 start=(n == 0 and k == 0), stop=(n == 2 and k == K - 1))
                        return last

                    def tick(t):
                        b = t - 1
                        if b.within(0, B1):
                            pe.wait_ge(p_ready, (b + 1).v)
                            if b >= 1:
                                pe.wait_ge(pT_lo_ready, b.v)
                            transpose(pT_ps, p).then_inc(pT_ready, 1)
                        b = t
                        if b.within(0, B1):
                            e = expert_of(b)
                            pe.wait_ge(hT_lo_ready, (b + 1).v)
                            if b >= 2:
                                pe.wait_ge(p_ready, (b - 1).v)
                            if b.turn is None and b.first < T1_LOOP:
                                pe.wait_ge(ctx_lo_ready, e + 1)
                            product(a_ps[b % 2], hT_hi, hT_lo, e).then_inc(a_ready, 1)
                        m = t + (1 + EARLY)
                        if m.within(EARLY - 1, MATS):
                            sum_mean(m)
                        b = t - 2
                        if b.within(0, B1):
                            pe.wait_ge(x1_ready, (b + 1).v)
                            if b >= 1:
                                pe.wait_ge(x1T_copied, b.v)
                            transpose(x1T_ps, row[b % 2]).then_inc(x1T_ready, 1)
                        b = t + 1
                        if b.within(0, B1):
                            pe.wait_ge(h_ready, (b + 1).v)
                            if b >= 1:
                                pe.wait_ge(hT_lo_ready, b.v)
                            transpose(hT_ps, h).then_inc(hT_ready, 1)
                        b = t - 1
                        if b.within(0, B1):
                            e = expert_of(b)
                            pe.wait_ge(pT_lo_ready, (b + 1).v)
                            if b >= 1:
                                pe.wait_ge(x1_ready, b.v)
                            product(y_ps, pT_hi, pT_lo, e).then_inc(y_ready, 1)
                        b = t - 2
                        if b.within(0, B1):
                            pe.wait_ge(x1T_copied, (b + 1).v)
                            if b >= 1:
                                pe.wait_ge(routed, (b * 2).v)
                            for k in range(K):
                                last = pe.matmul(logits_ps[:, 0:E2], x1T[:, k * P:(k + 1) * P],
                                                 router[:, k * E2:(k + 1) * E2], start=(k == 0), stop=(k == K - 1))
                            last.then_inc(logits_ready, 1)

                    pe.wait_ge(sorted1, 1)
                    run_ticks(pe, T1_FIRST, T1_LAST, T1_LOOP, T1_UNROLL, T1_TURNS, tick)

            stack.pop()

        with ExitStack() as inner:
            stack.append(inner)
            row_hot2 = sb("row_hot2", [P, B1, P], F16)
            block_hot2 = sb("block_hot2", [P, B1, B2], F16)
            hots2 = (row_hot2, block_hot2)
            x1 = sb("x1_slots", [P, B2 * ROW], F32)
            t8 = sb("t8", [P, D], F32)
            qT = sb("qT", [P, D], BF16)
            relu = sb("relu", [P, D], F32)
            relu2 = sb("relu2", [P, D], F32)
            prod = [sb(f"prod{i}", [P, D], F32) for i in range(2)]
            r8 = sb("r8", [P, D], F32)
            rT = sb("rT", [P, D], BF16)
            fac = [sb(f"fac{i}", [P, 6], F32) for i in range(2)]
            magic = sb("magic", [P, 1], F32)
            gu_mean = sb("gu_mean", [P, E2], F32)
            gu_block = sb("gu_block", [P, B2], F32)
            d_block = sb("d_block", [P, B2], F32)
            out_scale = sb("out_scale", [P, B2], F32)
            is_expert = sb("is_expert", [P, B2], F32)

            x1_in = [sem(f"x1_in{i}") for i in range(2)]
            t8_ready, tT_ready, qT_ready = (sem(n) for n in ("t8_ready", "tT_ready", "qT_ready"))
            g_ready, u_ready, relu_ready, relu2_ready = (sem(n) for n in ("g_ready", "u_ready", "relu_ready", "relu2_ready"))
            prod_ready, factors, r8_ready, rT_ps_ready, rT_ready = (
                sem(n) for n in ("prod_ready", "factors", "r8_ready", "rT_ps_ready", "rT_ready"))
            d_ready, out_ready, out_done = sem("d_ready"), sem("out_ready"), sem("out_done")

            g_ps, u_ps = [bank[0], bank[1]], [bank[2], bank[3]]
            tT_ps, rT_ps, d_ps = bank[4], bank[5], bank[6]

            def row_of(b, first, n):
                return x1[:, bass.ds((b * ROW + first).v, n)]

            with nc.Block() as block:

                @block.gpsimd
                def _(pool):
                    pool.wait_ge(sorted2, 1)
                    for b in range(B2):
                        if b >= 2:
                            pool.wait_ge(x1_in[b % 2], 16 * (b // 2))
                        pool.indirect_dma_start(x1[:, b * ROW:(b + 1) * ROW], None, x1_rows,
                                                bass.IndirectOffsetOnAxis(ap=gather2[:, b:b + 1], axis=0),
                                                bounds_check=N - 1, oob_is_err=False).then_inc(x1_in[b % 2], 16)
                    for b in range(B2):
                        pool.wait_ge(out_ready, b + 1)
                        pool.indirect_dma_start(out, bass.IndirectOffsetOnAxis(ap=store2[:, b:b + 1], axis=0),
                                                x1[:, b * ROW:b * ROW + D], None,
                                                bounds_check=N - 1, oob_is_err=False).then_inc(out_done, 16)
                    pool.wait_ge(out_done, 16 * B2)

                @block.scalar
                def _(act):
                    def tick(t):
                        b = t - 2
                        if b.within(0, B2):
                            act.wait_ge(rT_ps_ready, (b + 1).v)
                            if b >= 1:
                                act.wait_ge(d_ready, b.v)
                            nc.scalar.activation(rT[:, :], rT_ps[:, :], ACT.Copy, bias=-MAGIC).then_inc(rT_ready, 1)
                        b = t - 1
                        if b.within(0, B2):
                            act.wait_ge(factors, (b * 6 + 6).v)
                            if b >= 1:
                                act.wait_ge(rT_ps_ready, b.v)
                            nc.scalar.activation(r8[:, :], prod[b % 2][:, :], ACT.Identity, bias=magic[:, :],
                                                 scale=fac[b % 2][:, 5:6]).then_inc(r8_ready, 1)
                        b = t
                        if b.within(0, B2):
                            act.wait_ge(g_ready, (b + 1).v)
                            nc.scalar.activation(relu[:, :], g_ps[b % 2][:, :], ACT.Relu).then_inc(relu_ready, 1)
                            act.wait_ge(relu_ready, (b + 1).v)
                            if b >= 1:
                                act.wait_ge(prod_ready, (b * 2).v)
                            nc.scalar.activation(relu2[:, :], relu[:, :], ACT.Square).then_inc(relu2_ready, 1)
                        b = t + 2
                        if b.within(0, B2):
                            act.wait_ge(x1_in[b % 2], ((b // 2) * 16 + 16).v)
                            if b >= 1:
                                act.wait_ge(tT_ready, b.v)
                            nc.scalar.activation(t8[:, :], row_of(b, 0, D), ACT.Identity, bias=row_of(b, OFFSET_COL, 1),
                                                 scale=row_of(b, SCALE_COL, 1)).then_inc(t8_ready, 1)

                    run_ticks(act, T2_FIRST, T2_LAST, T2_LOOP, T2_UNROLL, T2_TURNS, tick)

                @block.vector
                def _(dve):
                    chain = sem("chain2")
                    count = [0]

                    def link(ins):
                        count[0] += 1
                        ins.then_inc(chain, 1)
                        dve.wait_ge(chain, count[0])

                    member3 = member2[:, :].rearrange("p (e t) -> p e t", e=E2)
                    wide = [P, E2, B1]
                    link(dve.tensor_tensor(member3, iota[:, 0:E2, None].to_broadcast(wide),
                                           choice[:, None, :].to_broadcast(wide), ALU.is_equal))
                    link(dve.tensor_tensor(member3, member3, valid1[:, None, :].to_broadcast(wide), ALU.mult))
                    def last_weights():
                        last = MATS - 1
                        dve.wait_ge(tern_act, MATS)
                        cols = slice(last * K * D, MATS * K * D)
                        dve.tensor_scalar(ternary[:, cols], ternary[:, cols].bitcast(I16), 1.0, -1.0,
                                          ALU.min, ALU.max).then_inc(tern, 1)
                        dve.memset(magic[:, :], MAGIC)
                        means = w_mean[:, :].rearrange("p (e k) -> p k e", k=3)
                        link(dve.tensor_tensor(gu_mean[:, :], means[:, 0, :], means[:, 0, :], ALU.mult))
                        link(dve.tensor_tensor(gu_mean[:, :], gu_mean[:, :], means[:, 1, :], ALU.mult))

                    sort_vector(dve, link, member2, E2, B1, B2, table1, expert2, gather2, store2, hots2, 1,
                                last_weights)
                    link(dve.memset(gu_block[:, :], 0.0))
                    link(dve.memset(d_block[:, :], 0.0))
                    for e in range(E2):
                        link(dve.tensor_scalar(is_expert[:, :], expert_f[:, 0:B2], float(e), None, ALU.is_equal))
                        dve.scalar_tensor_tensor(gu_block[:, :], is_expert[:, :], gu_mean[:, e:e + 1], gu_block[:, :],
                                                 ALU.mult, ALU.add)
                        link(dve.scalar_tensor_tensor(d_block[:, :], is_expert[:, :], w_mean[:, 3 * e + 2:3 * e + 3],
                                                      d_block[:, :], ALU.mult, ALU.add))

                    def tick(t):
                        b = t - 3
                        if b.within(0, B2):
                            dve.wait_ge(d_ready, (b + 1).v)
                            dve.wait_ge(factors, (b * 6 + 6).v)
                            dve.scalar_tensor_tensor(row_of(b, 0, D), d_ps[:, :], out_scale[:, bass.ds(b.v, 1)], row_of(b, 0, D),
                                                     ALU.mult, ALU.add).then_inc(out_ready, 1)
                        b = t + 1
                        if b.within(0, B2):
                            dve.wait_ge(tT_ready, (b + 1).v)
                            if b >= 1:
                                dve.wait_ge(u_ready, b.v)
                            dve.tensor_scalar(qT[:, :], tT_ps[:, :], MAGIC, MAGIC, ALU.add, ALU.subtract)\
                                .then_inc(qT_ready, 1)
                        b = t
                        if b.within(0, B2):
                            f = fac[b % 2]
                            dve.wait_ge(u_ready, (b + 1).v)
                            dve.wait_ge(relu2_ready, (b + 1).v)
                            if b >= 2:
                                dve.wait_ge(r8_ready, (b - 1).v)
                            dve.tensor_tensor(prod[b % 2][:, :], u_ps[b % 2][:, :], relu2[:, :], ALU.mult)\
                                .then_inc(prod_ready, 1)
                            dve.wait_ge(prod_ready, (b * 2 + 1).v)
                            dve.tensor_reduce(f[:, 0:1], prod[b % 2][:, :], X, ALU.max, apply_absolute_value=True)\
                                .then_inc(prod_ready, 1)
                            dve.tensor_scalar(f[:, 1:2], row_of(b, CUBE_COL, 1), gu_block[:, bass.ds(b.v, 1)], None,
                                              ALU.mult).then_inc(factors, 1)
                            dve.wait_ge(factors, (b * 6 + 1).v)
                            dve.wait_ge(prod_ready, (b * 2 + 2).v)
                            dve.tensor_scalar(f[:, 2:3], f[:, 0:1], f[:, 1:2], EPS, ALU.mult, ALU.max)\
                                .then_inc(factors, 1)
                            dve.wait_ge(factors, (b * 6 + 2).v)
                            dve.tensor_scalar(f[:, 3:4], f[:, 2:3], 1.0 / QMAX, None, ALU.mult).then_inc(factors, 1)
                            dve.wait_ge(factors, (b * 6 + 3).v)
                            dve.reciprocal(f[:, 4:5], f[:, 3:4]).then_inc(factors, 1)
                            dve.wait_ge(factors, (b * 6 + 4).v)
                            dve.tensor_scalar(out_scale[:, bass.ds(b.v, 1)], f[:, 3:4], d_block[:, bass.ds(b.v, 1)], None,
                                              ALU.mult).then_inc(factors, 1)
                            dve.tensor_scalar(f[:, 5:6], f[:, 1:2], f[:, 4:5], None, ALU.mult).then_inc(factors, 1)

                    run_ticks(dve, T2_FIRST, T2_LAST + 1, T2_LOOP, T2_UNROLL, T2_TURNS, tick)

                @block.tensor
                def _(pe):
                    sort_tensor(pe, member2, E2, B1, B2, hots2, -(-TILES // HOT_CHUNK), 1)

                    def transpose(ps, src):
                        for k in range(K):
                            last = pe.transpose(ps[:, k * P:(k + 1) * P], src[:, k * P:(k + 1) * P], ident[:, :])
                        return last

                    def product(ps, left, e, kind):
                        for k in range(K):
                            last = pe.matmul(ps[:, :], left[:, k * P:(k + 1) * P],
                                             ternary[:, bass.ds(e * (3 * K * D) + (kind * K + k) * D, D)],
                                             start=(k == 0), stop=(k == K - 1))
                        return last

                    def tick(t):
                        b = t - 2
                        if b.within(0, B2):
                            pe.wait_ge(r8_ready, (b + 1).v)
                            if b >= 1:
                                pe.wait_ge(rT_ready, b.v)
                            transpose(rT_ps, r8).then_inc(rT_ps_ready, 1)
                        b = t
                        if b.within(0, B2):
                            e = pe.value_load(expert2[0:1, bass.ds(b.v, 1)], min_val=0, max_val=E2 - 1)
                            pe.wait_ge(qT_ready, (b + 1).v)
                            if b >= 2:
                                pe.wait_ge(prod_ready, (b * 2 - 3).v)
                            product(g_ps[b % 2], qT, e, 0).then_inc(g_ready, 1)
                            product(u_ps[b % 2], qT, e, 1).then_inc(u_ready, 1)
                        b = t + 1
                        if b.within(0, B2):
                            pe.wait_ge(t8_ready, (b + 1).v)
                            if b >= 1:
                                pe.wait_ge(qT_ready, b.v)
                            transpose(tT_ps, t8).then_inc(tT_ready, 1)
                        b = t - 2
                        if b.within(0, B2):
                            e = pe.value_load(expert2[0:1, bass.ds(b.v, 1)], min_val=0, max_val=E2 - 1)
                            pe.wait_ge(rT_ready, (b + 1).v)
                            if b >= 1:
                                pe.wait_ge(out_ready, b.v)
                            product(d_ps, rT, e, 2).then_inc(d_ready, 1)

                    pe.wait_ge(sorted2, 1)
                    pe.wait_ge(tern, 4 * MATS)
                    run_ticks(pe, T2_FIRST, T2_LAST, T2_LOOP, T2_UNROLL, T2_TURNS, tick)

            stack.pop()


def kernel(x, itok_BxS_13_99985, ctx_2048, L0_ffn_router_w, L0_ffn_wg, L0_ffn_wu, L0_ffn_wd):
    import numpy as np
    import concourse.bacc as bacc
    from concourse.bass_utils import run_bass_kernel_spmd

    def chunked(w):
        n = w.shape[0]
        w = w.transpose(0, 2, 1).reshape(n, K, P, w.shape[1])
        return np.ascontiguousarray(w.transpose(0, 2, 1, 3).reshape(n, P, -1))

    wg, wu, wd = (np.asarray(w) for w in (L0_ffn_wg, L0_ffn_wu, L0_ffn_wd))
    arrays = {
        "x_rows": np.ascontiguousarray(np.asarray(x).reshape(N, D)),
        "token_ids_in": np.ascontiguousarray(np.asarray(itok_BxS_13_99985).reshape(TILES, P).T),
        "ctx_chunks": chunked(np.asarray(ctx_2048)),
        "router_chunks": chunked(np.asarray(L0_ffn_router_w)[None])[0],
        "weight_chunks": chunked(np.stack([wg, wu, wd], axis=1).reshape(MATS, D, D)),
    }
    nc = bacc.Bacc("TRN2", target_bir_lowering=False, num_devices=1, dynamic_dma_scratch_size=4096)
    args = [nc.dram_tensor(name, a.shape, mybir.dt.from_np(a.dtype), kind="ExternalInput").ap()
            for name, a in arrays.items()]
    out = nc.dram_tensor("out_rows", (N, D), F32, kind="ExternalOutput").ap()
    moe_program(nc, *args, out)
    r = run_bass_kernel_spmd(nc, [arrays], core_ids=[0])
    return np.asarray(r.results[0]["out_rows"]).reshape(np.asarray(x).shape)
```

```python
from contextlib import ExitStack

import concourse.bass as bass
from concourse import mybir

ALU = mybir.AluOpType
ACT = mybir.ActivationFunctionType
X = mybir.AxisListType.X
F32 = mybir.dt.float32
F32R = mybir.dt.float32r
BF16 = mybir.dt.bfloat16
F16 = mybir.dt.float16
I16 = mybir.dt.int16
I32 = mybir.dt.int32
U32 = mybir.dt.uint32

P = 128
N = 2048
D = 512
K = D // P
TILES = N // P
E1, E2 = 4, 8
B1 = TILES + E1 - 1
B2 = TILES + E2 - 1
MATS = 3 * E2
ID_STEP = 25000 // E1
EPS = 1e-5
QMAX = 127.0
MAGIC = 12582912.0
ROW = D + 4
SCALE_COL, OFFSET_COL, STEP_COL, CUBE_COL = range(D, D + 4)
LATE = 2
MADE = 10
DVE_COLS = 1024
RING = 4
WARM_UP1, WARM_UP2 = 20, 9


class At:

    def __init__(self, first, stride=0, turn=None):
        self.first, self.stride, self.turn = first, stride, turn

    def __add__(self, n):
        return At(self.first + n, self.stride, self.turn)

    def __sub__(self, n):
        return self + -n

    def __mul__(self, n):
        return At(self.first * n, self.stride * n, self.turn)

    def __floordiv__(self, n):
        assert self.stride % n == 0
        return At(self.first // n, self.stride // n, self.turn)

    def __mod__(self, n):
        assert self.stride % n == 0
        return self.first % n

    def __ge__(self, n):
        return self.first >= n

    @property
    def v(self):
        return self.first if self.turn is None else self.turn * self.stride + self.first

    def within(self, low, high, turns=1):
        if self.turn is not None:
            assert low <= self.first, (low, self.first)
            return True
        return low <= self.first < high


def run_ticks(eng, first, last, loop_first, unroll, turns, tick):
    for t in range(first, loop_first):
        tick(At(t))
    with eng.Fori(0, turns) as turn:
        for u in range(unroll):
            tick(At(loop_first + u, unroll, turn))
    for t in range(loop_first + unroll * turns, last + 1):
        tick(At(t))


T1_FIRST, T1_LAST, T1_LOOP, T1_UNROLL, T1_TURNS = -2, B1 + 2, 5, 4, 3
T2_FIRST, T2_LAST, T2_LOOP, T2_UNROLL, T2_TURNS = -2, B2 + 3, 4, 8, 2
assert T1_LOOP + T1_UNROLL * T1_TURNS + 1 <= B1
assert T2_LOOP + T2_UNROLL * T2_TURNS + 2 <= B2


def moe_program(nc, x_in, tokens_in, ctx_in, router_in, weights_in, out):
    with ExitStack() as whole:
        stack = [whole]

        def sb(name, shape, dt):
            return stack[-1].enter_context(nc.sbuf_tensor(name, shape, dt))

        def sem(name):
            return whole.enter_context(nc.semaphore(name))

        x1_rows = nc.dram_tensor("x1_rows", [N, ROW], F32).ap()

        bank = [whole.enter_context(nc.psum_tensor(f"bank{i}", [P, D], F32)) for i in range(8)]

        ternary = sb("ternary", [P, MATS * K * D], BF16)
        ident = sb("ident", [P, P], F32)
        ident16 = sb("ident16", [P, P], BF16)
        before = sb("before", [P, P], F32)
        ones = sb("ones", [P, P], F32)
        iota_i = sb("iota_i", [P, P], I32)
        iota = sb("iota", [P, P], F32)
        iota16 = sb("iota16", [P, P], F16)
        half_powers = sb("half_powers", [P, 2], F32)
        token1 = sb("token1", [P, TILES], F32)
        token1_i = sb("token1_i", [P, TILES], I32)
        token_ids = sb("token_ids", [P, TILES], I32)
        at_least = sb("at_least", [P, (E1 + 1) * TILES], F32)
        member1 = sb("member1", [P, E1 * TILES], F32)
        member2 = sb("member2", [P, E2 * B1], F32)
        scan = sb("scan", [P, E2 * B2], F32)
        earlier = sb("earlier", [P, E2 * B1], F32)
        placed = sb("placed", [P, E2 * B2], F32)
        place = sb("place", [P, B1], F32)
        place_block = sb("place_block", [P, B1], F32)
        place_row = sb("place_row", [P, B1], F32)
        small = sb("small", [P, 10, E2], F32)
        table1 = sb("table1", [P, B1], F32)
        valid1 = sb("valid1", [P, B1], F32)
        choice = sb("choice", [P, B1], F32)
        pad = sb("pad", [P, B2], F32)
        gather1 = sb("gather1", [P, B1], I32)
        store1 = sb("store1", [P, B1], I32)
        gather2 = sb("gather2", [P, B2], I32)
        store2 = sb("store2", [P, B2], I32)
        expert_f = sb("expert_f", [P, B2], F32)
        expert1 = sb("expert1", [P, B1], I32)
        expert2 = sb("expert2", [P, B2], I32)
        router = sb("router", [P, K * E2], F32)
        router_sum = sb("router_sum", [P, E2], F32)
        abs_sum = sb("abs_sum", [P, MATS], F32)
        w_mean = sb("w_mean", [P, MATS], F32)
        w_scale = sb("w_scale", [P, MATS], F32)

        inputs_in = sem("inputs_in")
        made = sem("made")
        pool_passed, dve_passed = sem("pool_passed"), sem("dve_passed")
        sorting = sem("sorting")
        sort_pe = sem("sort_pe")
        placing, hot_ready = sem("placing"), sem("hot_ready")
        sorted1, sorted2 = sem("sorted1"), sem("sorted2")
        pool_hot_ready = sem("pool_hot_ready")
        experts_ready = sem("experts_ready")
        sorted_sem = (sorted1, sorted2)

        def sort_vector(dve, link, member, n_exp, n_tiles, n_blocks, tokens, experts, gather, store, hots, lap,
                        meanwhile, before_rows):
            width = n_exp * n_tiles
            m = member[:, 0:width]
            m3 = m.rearrange("p (e t) -> p e t", e=n_exp)
            blocks, blocks_sum, excess, excess_sum, start, lift, part = (small[:, i, 0:n_exp] for i in range(7))
            count_ps = bank[7][:, 256:256 + n_exp]
            dve.tensor_reduce(part, m3, X, ALU.add)
            link(dve.tensor_tensor_scan(scan[:, 0:width], ones_wide[:, 0:width], m, 0.0, ALU.mult, ALU.add))
            link(dve.tensor_tensor(earlier[:, 0:width], scan[:, 0:width], m, ALU.subtract))
            dve.sem_inc(sorting, 1)
            meanwhile()
            dve.wait_ge(sort_pe, 2 * lap + 1)
            link(dve.tensor_scalar(blocks, count_ps, 1.0 / P, 0.5 - 0.5 / P, ALU.mult, ALU.add))
            link(dve.tensor_scalar(blocks, blocks, MAGIC, MAGIC, ALU.add, ALU.subtract))
            link(dve.scalar_tensor_tensor(excess, blocks, float(P), count_ps, ALU.mult, ALU.subtract))
            dve.tensor_tensor_scan(blocks_sum, ones[:, 0:n_exp], blocks, 0.0, ALU.mult, ALU.add)
            link(dve.tensor_tensor_scan(excess_sum, ones[:, 0:n_exp], excess, 0.0, ALU.mult, ALU.add))
            dve.tensor_tensor(start, blocks_sum, blocks, ALU.subtract)
            link(dve.tensor_tensor(lift, excess_sum, excess, ALU.subtract))
            wide = [P, n_exp, n_tiles]
            rank3 = bank[7][:, 0:width].rearrange("p (e t) -> p e t", e=n_exp)
            placed3 = placed[:, 0:width].rearrange("p (e t) -> p e t", e=n_exp)
            link(dve.tensor_tensor(placed3, rank3, small[:, 5, 0:n_exp, None].to_broadcast(wide), ALU.add))
            link(dve.tensor_tensor(placed3, placed3, m3, ALU.mult))
            link(dve.tensor_reduce(place[:, 0:n_tiles], placed[:, 0:width].rearrange("p (e t) -> p t e", e=n_exp),
                                   X, ALU.add))
            link(dve.tensor_scalar(place_block[:, 0:n_tiles], place[:, 0:n_tiles], 1.0 / P, 0.5 / P - 0.5,
                                   ALU.mult, ALU.add))
            link(dve.tensor_scalar(place_block[:, 0:n_tiles], place_block[:, 0:n_tiles], MAGIC, MAGIC,
                                   ALU.add, ALU.subtract))
            dve.scalar_tensor_tensor(place_row[:, 0:n_tiles], place_block[:, 0:n_tiles], -float(P),
                                     place[:, 0:n_tiles], ALU.mult, ALU.add).then_inc(placing, 1)
            row_hot, block_hot = hots
            wide = [P, n_tiles, n_blocks]
            link(dve.tensor_tensor(block_hot[:, :, 0:n_blocks], iota[:, None, 0:n_blocks].to_broadcast(wide),
                                   place_block[:, 0:n_tiles, None].to_broadcast(wide), ALU.is_equal))
            dve.tensor_tensor(block_hot[:, :, 0:n_blocks], block_hot[:, :, 0:n_blocks],
                              tokens[:, 0:n_tiles, None].to_broadcast(wide), ALU.mult)
            before_rows()
            dve.wait_ge(placing, lap + 1)
            for t in range(pool_tiles(n_tiles), n_tiles):
                dve.tensor_scalar(row_hot[:, t, :], iota16[:, :], place_row[:, t:t + 1], None, ALU.is_equal)\
                    .then_inc(hot_ready, 1)
            table_ps = bank[6][:, 0:n_blocks]
            dve.wait_ge(sort_pe, 2 * lap + 2)
            link(dve.tensor_scalar(pad[:, 0:n_blocks], table_ps, 0.0, None, ALU.is_equal))
            link(dve.scalar_tensor_tensor(gather[:, 0:n_blocks], table_ps, -1.0, pad[:, 0:n_blocks],
                                          ALU.add, ALU.add))
            dve.sem_inc(sorted_sem[lap], 1)
            wide = [P, n_blocks, n_exp - 1]
            started = scan[:, 0:n_blocks * (n_exp - 1)].rearrange("p (b e) -> p b e", b=n_blocks)
            link(dve.tensor_tensor(started, iota[:, 0:n_blocks, None].to_broadcast(wide),
                                   small[:, 4:5, 1:n_exp].to_broadcast(wide), ALU.is_ge))
            link(dve.tensor_reduce(expert_f[:, 0:n_blocks], started, X, ALU.add))
            link(dve.tensor_copy(experts[:, 0:n_blocks], expert_f[:, 0:n_blocks]))
            dve.sem_inc(experts_ready, 1)
            link(dve.scalar_tensor_tensor(pad[:, 0:n_blocks], pad[:, 0:n_blocks], float(2 * N), table_ps,
                                          ALU.mult, ALU.add))
            link(dve.tensor_scalar(store[:, 0:n_blocks], pad[:, 0:n_blocks], -1.0, None, ALU.add))

        def pool_tiles(n_tiles):
            return n_tiles * 2 // 7

        def sort_pool(pool, n_tiles, hots, lap):
            pool.wait_ge(placing, lap + 1)
            for t in range(pool_tiles(n_tiles)):
                pool.tensor_scalar(hots[0][:, t, :], iota16[:, :], place_row[:, t:t + 1], None, ALU.is_equal)\
                    .then_inc(pool_hot_ready, 1)

        def warm_up(pe, n):
            for _ in range(n):
                pe.matmul(bank[3][:, :], iota16[:, :], iota16[:, None, :].to_broadcast([P, K, P]), start=True, stop=True)

        def sort_tensor(pe, member, n_exp, n_tiles, n_blocks, hots, tiles_before, lap, meanwhile):
            width = n_exp * n_tiles
            pe.wait_ge(sorting, lap + 1)
            pe.matmul(bank[7][:, 0:width], before[:, :], member[:, 0:width], start=True, stop=False)
            pe.matmul(bank[7][:, 0:width], ones[:, 0:P], earlier[:, 0:width], start=False, stop=True)
            pe.matmul(bank[7][:, 256:256 + n_exp], ones[:, 0:P], small[:, 6, 0:n_exp], start=True,
                      stop=True).then_inc(sort_pe, 1)
            meanwhile()
            row_hot, block_hot = hots
            n_pool = pool_tiles(n_tiles)
            for i in range(n_tiles - n_pool):
                pe.wait_ge(hot_ready, tiles_before - pool_tiles(tiles_before) + i + 1)
                last = pe.matmul(bank[6][:, 0:n_blocks], row_hot[:, n_pool + i, :], block_hot[:, n_pool + i, 0:n_blocks],
                                 start=(i == 0), stop=(i >= n_pool and i == n_tiles - n_pool - 1))
                if i < n_pool:
                    pe.wait_ge(pool_hot_ready, pool_tiles(tiles_before) + i + 1)
                    last = pe.matmul(bank[6][:, 0:n_blocks], row_hot[:, i, :], block_hot[:, i, 0:n_blocks],
                                     start=False, stop=(i == n_tiles - n_pool - 1))
            last.then_inc(sort_pe, 1)

        ones_wide = sb("ones_wide", [P, E2 * B1], F32)
        staged = [sb(f"staged{i}", [P, K * D], F32) for i in range(2)]
        staged_in = [sem(f"staged_in{i}") for i in range(2)]
        table_read, late = sem("table_read"), sem("late")
        row_out = [sem(f"row_out{i}") for i in range(2)]
        abs_ready, mean_ready, tern, tern_act = (sem(n) for n in ("abs_ready", "mean_ready", "tern", "tern_act"))
        mean_ps = bank[6]

        def nothing():
            pass

        def step_inverse(dve, b):
            dve.wait_ge(step_ready, (b * 2 + 2).v)
            dve.reciprocal(ln2[b % 2][:, 8:9], row[b % 2][:, STEP_COL:STEP_COL + 1]).then_inc(step_inv, 1)

        def mean_of(dve, m):
            one = bass.ds(m.v, 1)
            dve.wait_ge(mean_ready, (m + 1).v)
            dve.tensor_scalar(w_mean[:, one], mean_ps[:, bass.ds((m + 64).v, 1)], 1.0 / (D * D), EPS,
                              ALU.mult, ALU.max).then_inc(tern, 1)

        def scale_of(dve, m):
            one = bass.ds(m.v, 1)
            dve.wait_ge(tern, (m * 4 + 1).v)
            dve.reciprocal(w_scale[:, one], w_mean[:, one]).then_inc(tern, 1)

        def scale_part(dve, m):
            one = bass.ds(m.v, 1)
            dve.wait_ge(tern, (m * 4 + 2).v)
            dve.tensor_scalar(ternary[:, bass.ds((m * (K * D)).v, DVE_COLS)].bitcast(I16),
                              staged[m % 2][:, 0:DVE_COLS], w_scale[:, one], None,
                              ALU.mult).then_inc(tern, 1)

        def sum_abs(m):
            nc.scalar.wait_ge(staged_in[m % 2], ((m // 2) * 16 + 16).v)
            nc.scalar.activation(ternary[:, bass.ds((m * (K * D)).v, K * D)], staged[m % 2][:, :], ACT.Abs,
                                 accum_out=abs_sum[:, bass.ds(m.v, 1)]).then_inc(abs_ready, 1)

        def sum_mean(pe, m):
            pe.wait_ge(abs_ready, (m + 1).v)
            if m >= 1:
                pe.wait_ge(tern, (m * 4 - 3).v)
            else:
                pe.wait_ge(table_read, 1)
            pe.matmul(mean_ps[:, bass.ds((m + 64).v, 1)], ones[:, 0:P], abs_sum[:, bass.ds(m.v, 1)],
                      start=True, stop=True).then_inc(mean_ready, 1)

        def cut(dve, m, scaled):
            cols = bass.ds((m * (K * D)).v, K * D)
            dve.wait_ge(tern, scaled.v)
            dve.wait_ge(tern_act, (m + 1).v)
            dve.tensor_scalar(ternary[:, cols], ternary[:, cols].bitcast(I16), 1.0, -1.0,
                              ALU.min, ALU.max).then_inc(tern, 1)

        block = whole.enter_context(nc.Block())

        with ExitStack() as inner:
            stack.append(inner)
            ctx_hi = sb("ctx_hi", [P, E1 * K * D], F32R)
            ctx_lo = sb("ctx_lo", [P, E1 * K * D], F32R)
            x = [sb(f"x{i}", [P, D], F32) for i in range(RING)]
            h = sb("h", [P, D], F32)
            hT_hi = sb("hT_hi", [P, D], F32R)
            hT_lo = sb("hT_lo", [P, D], F32R)
            sil = sb("sil", [P, D], F32)
            p = sb("p", [P, D], F32)
            pT_hi = sb("pT_hi", [P, D], F32R)
            pT_lo = sb("pT_lo", [P, D], F32R)
            row = [sb(f"row{i}", [P, ROW], F32) for i in range(2)]
            squares = sb("squares", [P, D], F32)
            x1T = sb("x1T", [P, D], F32)
            stats1 = sb("stats1", [P, 6], F32)
            mv1 = [sb(f"mv1_{i}", [P, 2], F32) for i in range(2)]
            ln1 = [sb(f"ln1_{i}", [P, 3], F32) for i in range(2)]
            ln2 = [sb(f"ln2_{i}", [P, 9], F32) for i in range(2)]
            best = sb("best", [P, 8], F32)
            best_at = sb("best_at", [P, 8], U32)
            gather_at = [sb(f"gather_at{i}", [P, 1], I32) for i in range(RING)]
            store_at = [sb(f"store_at{i}", [P, 1], I32) for i in range(2)]

            def spare(matrix, n, dt):
                first = matrix * K * D
                return ternary[:, first:first + n].bitcast(dt)

            hots1 = (spare(12, TILES * P, F16).rearrange("p (t r) -> p t r", t=TILES),
                     spare(13, TILES * B2, F16).rearrange("p (t b) -> p t b", t=TILES))
            ctx_raw = [spare(16 + 2 * e, 2 * K * D, F32) for e in range(E1)]

            ctx_in_sem = [sem(f"ctx_in{e}") for e in range(E1)]
            ctx_hi_ready, ctx_lo_ready = sem("ctx_hi_ready"), sem("ctx_lo_ready")
            gather_at_ready, store_at_ready = sem("gather_at_ready"), sem("store_at_ready")
            x_in_sem = [sem(f"x_in{i}") for i in range(RING)]
            moments1 = sem("moments1")
            norm1 = sem("norm1")
            h_ready, hT_ready, hT_hi_ready, hT_lo_ready = (sem(n) for n in ("h_ready", "hT_ready", "hT_hi_ready", "hT_lo_ready"))
            a_ready, sil_ready, p_ready = (sem(n) for n in ("a_ready", "sil_ready", "p_ready"))
            pT_ready, pT_hi_ready, pT_lo_ready = (sem(n) for n in ("pT_ready", "pT_hi_ready", "pT_lo_ready"))
            y_ready, x1_ready, mean2_ready, norm2 = (sem(n) for n in ("y_ready", "x1_ready", "mean2_ready", "norm2"))
            squares_ready, x1T_ready, x1T_copied, logits_ready = (sem(n) for n in ("squares_ready", "x1T_ready", "x1T_copied", "logits_ready"))
            largest_ready, step_ready, step_inv, quant_ready = (sem(n) for n in ("largest_ready", "step_ready", "step_inv", "quant_ready"))
            routed, chosen = sem("routed"), sem("chosen")
            router_sum_ready, router_mean_ready, centred = (
                sem(n) for n in ("router_sum_ready", "router_mean_ready", "centred"))

            hT_ps, pT_ps, x1T_ps, y_ps = bank[0], bank[1], bank[2], bank[3]
            a_ps = [bank[4], bank[5]]
            logits_ps = bank[7]

            @block.sync
            def _(sp):
                sp.dma_start(token_ids[:, :], tokens_in).then_inc(inputs_in, 16)
                sp.dma_start(router[:, :], router_in).then_inc(inputs_in, 16)
                for e in range(E1):
                    sp.dma_start(ctx_raw[e], ctx_in[e]).then_inc(ctx_in_sem[e], 16)

                def load(m):
                    if m >= 2:
                        sp.wait_ge(tern, (m * 4 - 5).v)
                        sp.wait_ge(tern_act, (m - 1).v)
                    sp.dma_start(staged[m % 2][:, :], weights_in[bass.ds(m.v, 1)].rearrange("a p n -> (a p) n"))\
                      .then_inc(staged_in[m % 2], 16)

                sp.wait_ge(x_in_sem[0], 16)
                load(At(0))
                sp.wait_ge(x_in_sem[1], 16)
                load(At(1))
                with sp.Fori(0, MATS // 2 - 1) as turn:
                    for u in range(2):
                        load(At(2 + u, 2, turn))

            @block.gpsimd
            def _(pool):
                pool.iota(iota_i[:, :], [[1, P]], base=0, channel_multiplier=0).then_inc(made, 1)
                pool.iota(token1_i[:, :], [[P, TILES]], base=1, channel_multiplier=1).then_inc(made, 1)
                pool.memset(ones[:, :], 1.0).then_inc(made, 1)
                pool.memset(ones_wide[:, :], 1.0).then_inc(made, 1)
                pool.memset(before[:, :], 0.0).then_inc(made, 1)
                pool.memset(ident[:, :], 0.0).then_inc(made, 1)
                pool.memset(half_powers[:, 0:1], -0.5).then_inc(made, 1)
                pool.memset(half_powers[:, 1:2], 0.5).then_inc(made, 1)
                pool.wait_ge(made, 8)
                pool.affine_select(before[:, :], before[:, :], [[-1, P]], ALU.is_ge, 1.0, base=0,
                                   channel_multiplier=1).then_inc(made, 1)
                pool.affine_select(ident[:, :], ident[:, :], [[-1, P]], ALU.not_equal, 1.0, base=0,
                                   channel_multiplier=1).then_inc(made, 1)

                def gather(b):
                    if b >= RING:
                        pool.wait_ge(x1_ready, (b - (RING - 1)).v)
                        pool.sem_inc(pool_passed, 1)
                    pool.tensor_copy(gather_at[b % RING][:, :], gather1[:, bass.ds(b.v, 1)])\
                        .then_inc(gather_at_ready, 1)
                    pool.wait_ge(gather_at_ready, (b + 1).v)
                    pool.sem_inc(pool_passed, 1)
                    pool.indirect_dma_start(x[b % RING][:, :], None, x_in,
                                            bass.IndirectOffsetOnAxis(ap=gather_at[b % RING][:, :], axis=0),
                                            bounds_check=N - 1, oob_is_err=False)\
                        .then_inc(x_in_sem[b % RING], 16)

                def tick(t):
                    b = t + 1
                    if b.within(0, B1):
                        s = ln1[b % 2]
                        if b >= 2:
                            pool.wait_ge(h_ready, (b - 1).v)
                        pool.wait_ge(moments1, (b * 2 + 2).v)
                        pool.sem_inc(pool_passed, 1)
                        pool.tensor_scalar(s[:, 0:1], mv1[b % 2][:, 1:2], EPS, None, ALU.add).then_inc(norm1, 1)
                        pool.wait_ge(norm1, (b * 3 + 1).v)
                        pool.sem_inc(pool_passed, 1)
                        pool.tensor_tensor(s[:, 1:2], s[:, 0:1], half_powers[:, 0:1], ALU.pow).then_inc(norm1, 1)
                        pool.wait_ge(norm1, (b * 3 + 2).v)
                        pool.sem_inc(pool_passed, 1)
                        pool.tensor_scalar(s[:, 2:3], mv1[b % 2][:, 0:1], s[:, 1:2], -1.0, ALU.mult, ALU.mult)\
                            .then_inc(norm1, 1)
                    b = t - 3
                    if b.within(0, B1):
                        s, r = ln2[b % 2], row[b % 2]
                        pool.wait_ge(step_inv, (b + 1).v)
                        pool.sem_inc(pool_passed, 1)
                        pool.tensor_scalar(r[:, SCALE_COL:SCALE_COL + 1], s[:, 5:6], s[:, 8:9], None, ALU.mult)\
                            .then_inc(quant_ready, 1)
                        st = r[:, STEP_COL:STEP_COL + 1]
                        pool.tensor_scalar(r[:, CUBE_COL:CUBE_COL + 1], st, st, st, ALU.mult, ALU.mult)\
                            .then_inc(quant_ready, 1)
                        pool.wait_ge(quant_ready, (b * 3 + 1).v)
                        pool.sem_inc(pool_passed, 1)
                        pool.tensor_scalar(r[:, OFFSET_COL:OFFSET_COL + 1], r[:, SCALE_COL:SCALE_COL + 1],
                                           s[:, 1:2], None, ALU.mult).then_inc(quant_ready, 1)
                    b = t + 2
                    if b.within(RING, B1):
                        gather(b)
                    if t.turn is None and t.first == T1_FIRST + 1:
                        gather(At(2))
                        gather(At(3))
                    b = t - 3
                    if b.within(0, B1 - 1):
                        pool.wait_ge(routed, (b * 2 + 2).v)
                        pool.sem_inc(pool_passed, 1)
                        pool.tensor_copy(choice[:, bass.ds(b.v, 1)], best_at[:, 0:1]).then_inc(chosen, 1)
                    b = t - 3
                    if b.within(0, B1):
                        r = row[b % 2]
                        if b >= 2:
                            pool.wait_ge(row_out[b % 2], ((b // 2) * 16).v)
                            pool.sem_inc(pool_passed, 1)
                        pool.tensor_copy(store_at[b % 2][:, :], store1[:, bass.ds(b.v, 1)])\
                            .then_inc(store_at_ready, 1)
                        pool.wait_ge(store_at_ready, (b + 1).v)
                        pool.wait_ge(quant_ready, (b * 3 + 3).v)
                        pool.sem_inc(pool_passed, 1)
                        pool.indirect_dma_start(x1_rows, bass.IndirectOffsetOnAxis(ap=store_at[b % 2][:, :], axis=0),
                                                r[:, :], None, bounds_check=N - 1, oob_is_err=False)\
                            .then_inc(row_out[b % 2], 16)
                    b = t - 2
                    if b.within(0, B1):
                        s = ln2[b % 2]
                        pool.wait_ge(squares_ready, (b + 1).v)
                        pool.sem_inc(pool_passed, 1)
                        pool.tensor_scalar(s[:, 3:4], s[:, 2:3], 1.0 / D, EPS, ALU.mult, ALU.add).then_inc(norm2, 1)
                        pool.wait_ge(norm2, (b * 2 + 1).v)
                        pool.wait_ge(largest_ready, (b + 1).v)
                        pool.sem_inc(pool_passed, 1)
                        pool.tensor_tensor(s[:, 5:7], s[:, 3:5], half_powers[:, :], ALU.pow).then_inc(norm2, 1)
                        pool.wait_ge(norm2, (b * 2 + 2).v)
                        pool.sem_inc(pool_passed, 1)
                        pool.tensor_scalar(s[:, 7:8], s[:, 6:7], s[:, 5:6], None, ALU.mult).then_inc(step_ready, 1)
                        pool.wait_ge(step_ready, (b * 2 + 1).v)
                        pool.sem_inc(pool_passed, 1)
                        pool.tensor_scalar(row[b % 2][:, STEP_COL:STEP_COL + 1], s[:, 7:8], EPS, 1.0 / QMAX,
                                           ALU.max, ALU.mult).then_inc(step_ready, 1)

                sort_pool(pool, TILES, hots1, 0)
                pool.wait_ge(sorted1, 1)
                for b in range(2):
                    gather(At(b))
                run_ticks(pool, T1_FIRST, T1_LAST, T1_LOOP, T1_UNROLL, T1_TURNS, tick)

            @block.scalar
            def _(act):
                act.preload_act_table(ACT.Silu)
                for e in range(E1):
                    act.wait_ge(ctx_in_sem[e], 16)
                    nc.scalar.activation(ctx_hi[:, e * K * D:(e + 1) * K * D], ctx_raw[e], ACT.Copy)\
                        .then_inc(ctx_hi_ready, 1)

                def scale_part(m):
                    act.wait_ge(tern, (m * 4 + 2).v)
                    nc.scalar.activation(
                        ternary[:, bass.ds((m * (K * D) + DVE_COLS).v, K * D - DVE_COLS)].bitcast(I16),
                        staged[m % 2][:, DVE_COLS:], ACT.Copy, scale=w_scale[:, bass.ds(m.v, 1)])\
                        .then_inc(tern_act, 1)

                def tick(t):
                    b = t - 1
                    if b.within(0, B1):
                        act.wait_ge(pT_ready, (b + 1).v)
                        nc.scalar.activation(pT_hi[:, :], pT_ps[:, :], ACT.Copy).then_inc(pT_hi_ready, 1)
                    b = t - 2
                    if b.within(0, B1):
                        act.wait_ge(mean2_ready, (b + 1).v)
                        if b >= 1:
                            act.wait_ge(largest_ready, b.v)
                        s = ln2[b % 2]
                        nc.scalar.activation(squares[:, :], row[b % 2][:, 0:D], ACT.Square, bias=s[:, 1:2],
                                             accum_out=s[:, 2:3]).then_inc(squares_ready, 1)
                    b = t + 1
                    if b.within(0, B1):
                        act.wait_ge(norm1, (b * 3 + 3).v)
                        if b >= 1:
                            act.wait_ge(hT_ready, b.v)
                        s = ln1[b % 2]
                        nc.scalar.activation(h[:, :], x[b % RING][:, :], ACT.Identity, bias=s[:, 2:3],
                                             scale=s[:, 1:2]).then_inc(h_ready, 1)
                    b = t
                    if b.within(0, B1):
                        act.wait_ge(a_ready, (b + 1).v)
                        if b >= 1:
                            act.wait_ge(p_ready, b.v)
                        nc.scalar.activation(sil[:, :], a_ps[b % 2][:, :], ACT.Silu).then_inc(sil_ready, 1)
                    b = t - 2
                    if b.within(0, B1):
                        act.wait_ge(x1T_ready, (b + 1).v)
                        if b >= 1:
                            act.wait_ge(logits_ready, b.v)
                        nc.scalar.activation(x1T[:, :], x1T_ps[:, :], ACT.Copy).then_inc(x1T_copied, 1)
                    b = t + 1
                    if b.within(0, B1):
                        act.wait_ge(hT_ready, (b + 1).v)
                        if b >= 1:
                            act.wait_ge(a_ready, b.v)
                        nc.scalar.activation(hT_hi[:, :], hT_ps[:, :], ACT.Copy).then_inc(hT_hi_ready, 1)
                    m = t
                    if m.within(0, MATS - LATE):
                        scale_part(m)
                    m = t + 1
                    if m.within(0, MATS):
                        sum_abs(m)

                run_ticks(act, T1_FIRST, T1_LAST, T1_LOOP, T1_UNROLL, T1_TURNS, tick)

            @block.vector
            def _(dve):
                chain = sem("chain1")
                count = [0]

                def link(ins):
                    count[0] += 1
                    ins.then_inc(chain, 1)
                    dve.wait_ge(chain, count[0])

                dve.wait_ge(made, MADE)
                dve.wait_ge(inputs_in, 32)
                dve.tensor_copy(iota[:, :], iota_i[:, :])
                dve.tensor_copy(iota16[:, :], iota_i[:, :])
                dve.tensor_copy(ident16[:, :], ident[:, :])
                link(dve.tensor_copy(token1[:, :], token1_i[:, :]))
                dve.memset(at_least[:, 0:TILES], 1.0)
                dve.memset(at_least[:, E1 * TILES:], 0.0)
                for e in range(1, E1):
                    last = dve.tensor_scalar(at_least[:, e * TILES:(e + 1) * TILES], token_ids[:, :],
                                             float(e * ID_STEP), None, ALU.is_ge)
                link(last)
                link(dve.tensor_tensor(member1[:, :], at_least[:, 0:E1 * TILES], at_least[:, TILES:], ALU.subtract))

                def centre_router():
                    router3 = router[:, :].rearrange("p (k e) -> p k e", k=K)
                    dve.wait_ge(router_mean_ready, 1)
                    link(dve.tensor_scalar(router_sum[:, :], logits_ps[:, 0:E2], 1.0 / D, None, ALU.mult))
                    dve.tensor_tensor(router3, router3, router_sum[:, None, :].to_broadcast([P, K, E2]),
                                      ALU.subtract).then_inc(centred, 1)

                dve.tensor_reduce(router_sum[:, :], router[:, :].rearrange("p (k e) -> p e k", k=K), X,
                                  ALU.add).then_inc(router_sum_ready, 1)
                sort_vector(dve, link, member1, E1, TILES, B1, token1, expert1, gather1, store1, hots1, 0,
                            centre_router, nothing)
                link(dve.tensor_copy(table1[:, :], bank[6][:, 0:B1]))
                dve.sem_inc(table_read, 1)
                link(dve.tensor_scalar(valid1[:, :], table1[:, :], 0.0, None, ALU.is_gt))

                def low_halves(e):
                    cols = slice(e * K * D, (e + 1) * K * D)
                    dve.wait_ge(ctx_hi_ready, e + 1)
                    dve.tensor_tensor(ctx_lo[:, cols], ctx_raw[e], ctx_hi[:, cols].bitcast(F32),
                                      ALU.subtract).then_inc(ctx_lo_ready, 1)

                def tick(t):
                    b = t - 2
                    if b.within(0, B1):
                        dve.wait_ge(y_ready, (b + 1).v)
                        if b >= 2:
                            dve.wait_ge(row_out[b % 2], ((b // 2) * 16).v)
                        dve.scalar_tensor_tensor(row[b % 2][:, 0:D], y_ps[:, :], 1.0, x[b % RING][:, :], ALU.mult,
                                                 ALU.add, accum_out=ln2[b % 2][:, 0:1]).then_inc(x1_ready, 1)
                    b = t - 3
                    if b.within(0, B1):
                        dve.wait_ge(logits_ready, (b + 1).v)
                        dve.sem_inc(dve_passed, 1)
                        dve.max(best[:, :], logits_ps[:, 0:E2]).then_inc(routed, 1)
                    b = t - 2
                    if b.within(0, B1):
                        dve.wait_ge(x1_ready, (b + 1).v)
                        dve.tensor_scalar(ln2[b % 2][:, 1:2], ln2[b % 2][:, 0:1], -1.0 / D, None, ALU.mult)\
                            .then_inc(mean2_ready, 1)
                    m = t - 1
                    if m.within(0, MATS - LATE - 1):
                        cut(dve, m, m * 4 + 3)
                    b = t - 3
                    if b.within(0, B1):
                        dve.wait_ge(routed, (b * 2 + 1).v)
                        if b >= 1:
                            dve.wait_ge(chosen, b.v)
                        dve.sem_inc(dve_passed, 1)
                        dve.max_index(best_at[:, :], best[:, :], logits_ps[:, 0:E2]).then_inc(routed, 1)
                    if t.turn is None and t.first == T1_LAST:
                        dve.wait_ge(routed, 2 * B1)
                        dve.tensor_copy(choice[:, B1 - 1:], best_at[:, 0:1]).then_inc(chosen, 1)
                    b = t - 1
                    if b.within(0, B1):
                        dve.wait_ge(pT_hi_ready, (b + 1).v)
                        if b >= 1:
                            dve.wait_ge(y_ready, b.v)
                        dve.tensor_tensor(pT_lo[:, :], pT_ps[:, :], pT_hi[:, :].bitcast(F32), ALU.subtract)\
                            .then_inc(pT_lo_ready, 1)
                    b = t - 2
                    if b.within(0, B1):
                        dve.wait_ge(squares_ready, (b + 1).v)
                        dve.tensor_reduce(ln2[b % 2][:, 4:5], squares[:, :], X, ALU.max).then_inc(largest_ready, 1)
                    m = t
                    if m.within(0, MATS - LATE - 1):
                        mean_of(dve, m)
                        scale_of(dve, m)
                    b = t
                    if b.within(0, B1):
                        dve.wait_ge(sil_ready, (b + 1).v)
                        if b >= 1:
                            dve.wait_ge(pT_ready, b.v)
                        dve.tensor_tensor(p[:, :], a_ps[b % 2][:, :], sil[:, :], ALU.mult).then_inc(p_ready, 1)
                    b = t + 1
                    if b.within(0, B1):
                        dve.wait_ge(hT_hi_ready, (b + 1).v)
                        dve.tensor_tensor(hT_lo[:, :], hT_ps[:, :], hT_hi[:, :].bitcast(F32), ALU.subtract)\
                            .then_inc(hT_lo_ready, 1)
                    b = t + 2
                    if b.within(0, B1):
                        dve.wait_ge(x_in_sem[b % RING], ((b // RING) * 16 + 16).v)
                        dve.bn_stats(stats1[:, :], x[b % RING][:, :]).then_inc(moments1, 1)
                    m = t
                    if m.within(0, MATS - LATE - 1):
                        scale_part(dve, m)
                    b = t + 2
                    if b.within(0, B1):
                        dve.wait_ge(moments1, (b * 2 + 1).v)
                        if b >= 2:
                            dve.wait_ge(norm1, (b * 3 - 3).v)
                        dve.sem_inc(dve_passed, 1)
                        dve.bn_aggr(mv1[b % 2][:, :], stats1[:, :]).then_inc(moments1, 1)
                    b = t - 2
                    if b.within(0, B1 - 1):
                        step_inverse(dve, b)

                low_halves(0)
                tick(At(T1_FIRST))
                low_halves(1)
                tick(At(T1_FIRST + 1))
                low_halves(2)
                low_halves(3)
                run_ticks(dve, T1_FIRST + 2, T1_LAST, T1_LOOP, T1_UNROLL, T1_TURNS, tick)

            @block.tensor
            def _(pe):
                pe.wait_ge(made, MADE)
                pe.wait_ge(router_sum_ready, 1)
                pe.matmul(logits_ps[:, 0:E2], ones[:, 0:P], router_sum[:, :], start=True,
                          stop=True).then_inc(router_mean_ready, 1)
                pe.wait_ge(centred, 1)
                sort_tensor(pe, member1, E1, TILES, B1, hots1, 0, 0, nothing)

                def transpose(ps, src):
                    for k in range(K):
                        last = pe.transpose(ps[:, k * P:(k + 1) * P], src[:, k * P:(k + 1) * P], ident[:, :])
                    return last

                def expert_of(b):
                    return pe.value_load(expert1[0:1, bass.ds(b.v, 1)], min_val=0, max_val=E1 - 1)

                def product(ps, hi, lo, e):
                    pairs = [(hi, ctx_hi), (hi, ctx_lo), (lo, ctx_hi)]
                    for n, (left, right) in enumerate(pairs):
                        for k in range(K):
                            last = pe.matmul(ps[:, :], left[:, k * P:(k + 1) * P],
                                             right[:, bass.ds(e * (K * D) + k * D, D)],
                                             start=(n == 0 and k == 0), stop=(n == 2 and k == K - 1))
                    return last

                def tick(t):
                    b = t - 1
                    if b.within(0, B1):
                        pe.wait_ge(p_ready, (b + 1).v)
                        if b >= 1:
                            pe.wait_ge(pT_lo_ready, b.v)
                        transpose(pT_ps, p).then_inc(pT_ready, 1)
                    b = t
                    if b.within(0, B1):
                        e = expert_of(b)
                        pe.wait_ge(hT_lo_ready, (b + 1).v)
                        if b >= 2:
                            pe.wait_ge(p_ready, (b - 1).v)
                        if b.turn is None and b.first < T1_LOOP:
                            pe.wait_ge(ctx_lo_ready, e + 1)
                        product(a_ps[b % 2], hT_hi, hT_lo, e).then_inc(a_ready, 1)
                    m = t
                    if m.within(0, MATS - LATE):
                        sum_mean(pe, m)
                    b = t - 2
                    if b.within(0, B1):
                        pe.wait_ge(x1_ready, (b + 1).v)
                        if b >= 1:
                            pe.wait_ge(x1T_copied, b.v)
                        transpose(x1T_ps, row[b % 2]).then_inc(x1T_ready, 1)
                    b = t + 1
                    if b.within(0, B1):
                        pe.wait_ge(h_ready, (b + 1).v)
                        if b >= 1:
                            pe.wait_ge(hT_lo_ready, b.v)
                        transpose(hT_ps, h).then_inc(hT_ready, 1)
                    b = t - 1
                    if b.within(0, B1):
                        e = expert_of(b)
                        pe.wait_ge(pT_lo_ready, (b + 1).v)
                        if b >= 1:
                            pe.wait_ge(x1_ready, b.v)
                        product(y_ps, pT_hi, pT_lo, e).then_inc(y_ready, 1)
                    b = t - 2
                    if b.within(0, B1):
                        pe.wait_ge(x1T_copied, (b + 1).v)
                        if b >= 1:
                            pe.wait_ge(routed, (b * 2).v)
                        for k in range(K):
                            last = pe.matmul(logits_ps[:, 0:E2], x1T[:, k * P:(k + 1) * P],
                                             router[:, k * E2:(k + 1) * E2], start=(k == 0), stop=(k == K - 1))
                        last.then_inc(logits_ready, 1)

                pe.wait_ge(experts_ready, 1)
                tick(At(T1_FIRST))
                warm_up(pe, WARM_UP1)
                run_ticks(pe, T1_FIRST + 1, T1_LAST, T1_LOOP, T1_UNROLL, T1_TURNS, tick)

            stack.pop()

        with ExitStack() as inner:
            stack.append(inner)
            row_hot2 = sb("row_hot2", [P, B1, P], F16)
            block_hot2 = sb("block_hot2", [P, B1, B2], F16)
            hots2 = (row_hot2, block_hot2)
            x1 = sb("x1_slots", [P, B2 * ROW], F32)
            t8 = [sb(f"t8_{i}", [P, D], I16) for i in range(2)]
            qT = [sb(f"qT{i}", [P, D], BF16) for i in range(2)]
            relu = sb("relu", [P, D], F32)
            relu2 = sb("relu2", [P, D], F32)
            prod = [sb(f"prod{i}", [P, D], F32) for i in range(2)]
            r8 = sb("r8", [P, D], I16)
            rT = [sb(f"rT{i}", [P, D], BF16) for i in range(2)]
            fac = [sb(f"fac{i}", [P, 6], F32) for i in range(2)]
            gu_mean = sb("gu_mean", [P, E2], F32)
            gu_block = sb("gu_block", [P, B2], F32)
            d_block = sb("d_block", [P, B2], F32)
            out_scale = sb("out_scale", [P, B2], F32)
            d_mean = sb("d_mean", [P, E2], F32)

            x1_in = [sem(f"x1_in{i}") for i in range(2)]
            t8_ready, tT_ready, qT_ready = (sem(n) for n in ("t8_ready", "tT_ready", "qT_ready"))
            g_ready, u_ready, relu_ready, relu2_ready = (sem(n) for n in ("g_ready", "u_ready", "relu_ready", "relu2_ready"))
            size_ready, amax_ready = sem("size_ready"), sem("amax_ready")
            prod_ready, factors, r8_ready, rT_ps_ready, rT_ready = (
                sem(n) for n in ("prod_ready", "factors", "r8_ready", "rT_ps_ready", "rT_ready"))
            d_ready, out_ready, out_done = sem("d_ready"), sem("out_ready"), sem("out_done")

            g_ps, u_ps = [bank[0], bank[1]], [bank[2], bank[3]]
            tT_ps = [bank[i][:, 0:D // 2].bitcast(BF16) for i in (4, 7)]
            rT_ps, d_ps = bank[5][:, 0:D // 2].bitcast(BF16), bank[6]

            def row_of(b, first, n):
                return x1[:, bass.ds((b * ROW + first).v, n)]

            @block.gpsimd
            def _(pool):
                sort_pool(pool, B1, hots2, 1)
                for i in range(2):
                    pool.wait_ge(row_out[i], 16 * ((B1 - i + 1) // 2))
                pool.wait_ge(sorted2, 1)
                for b in range(B2):
                    if b >= 2:
                        pool.wait_ge(x1_in[b % 2], 16 * (b // 2))
                    pool.indirect_dma_start(x1[:, b * ROW:(b + 1) * ROW], None, x1_rows,
                                            bass.IndirectOffsetOnAxis(ap=gather2[:, b:b + 1], axis=0),
                                            bounds_check=N - 1, oob_is_err=False).then_inc(x1_in[b % 2], 16)
                for b in range(B2):
                    pool.wait_ge(out_ready, b + 1)
                    pool.indirect_dma_start(out, bass.IndirectOffsetOnAxis(ap=store2[:, b:b + 1], axis=0),
                                            x1[:, b * ROW:b * ROW + D], None,
                                            bounds_check=N - 1, oob_is_err=False).then_inc(out_done, 16)
                pool.wait_ge(out_done, 16 * B2)

            @block.scalar
            def _(act):
                def late_part(i):
                    m = MATS - LATE + i
                    act.wait_ge(late, 2 * i + 2)
                    nc.scalar.activation(ternary[:, m * K * D:(m + 1) * K * D].bitcast(I16), staged[m % 2][:, :],
                                         ACT.Copy, scale=w_scale[:, m:m + 1]).then_inc(tern_act, 1)

                late_part(0)
                sum_abs(At(MATS - 1))
                late_part(1)

                def tick(t):
                    b = t + 2
                    if b.within(0, B2):
                        act.wait_ge(x1_in[b % 2], ((b // 2) * 16 + 16).v)
                        if b >= 2:
                            act.wait_ge(tT_ready, (b - 1).v)
                        nc.scalar.activation(t8[b % 2][:, :], row_of(b, 0, D), ACT.Identity,
                                             bias=row_of(b, OFFSET_COL, 1),
                                             scale=row_of(b, SCALE_COL, 1)).then_inc(t8_ready, 1)
                    b = t
                    if b.within(0, B2):
                        act.wait_ge(g_ready, (b + 1).v)
                        if b >= 1:
                            act.wait_ge(relu2_ready, b.v)
                        nc.scalar.activation(relu[:, :], g_ps[b % 2][:, :], ACT.Relu).then_inc(relu_ready, 1)
                        act.wait_ge(relu_ready, (b + 1).v)
                        if b >= 1:
                            act.wait_ge(prod_ready, b.v)
                        nc.scalar.activation(relu2[:, :], relu[:, :], ACT.Square).then_inc(relu2_ready, 1)
                    b = t - 2
                    if b.within(0, B2):
                        act.wait_ge(rT_ps_ready, (b + 1).v)
                        if b >= 2:
                            act.wait_ge(d_ready, (b - 1).v)
                        nc.scalar.activation(rT[b % 2][:, :], bank[5][:, 0:D // 2].bitcast(I16), ACT.Copy)\
                            .then_inc(rT_ready, 1)
                    b = t - 1
                    if b.within(0, B2):
                        act.wait_ge(factors, (b * 4 + 4).v)
                        if b >= 1:
                            act.wait_ge(rT_ps_ready, b.v)
                        nc.scalar.activation(r8[:, :], prod[b % 2][:, :], ACT.Copy,
                                             scale=fac[b % 2][:, 3:4]).then_inc(r8_ready, 1)

                run_ticks(act, T2_FIRST, T2_LAST, T2_LOOP, T2_UNROLL, T2_TURNS, tick)

            @block.vector
            def _(dve):
                chain = sem("chain2")
                count = [0]

                def link(ins):
                    count[0] += 1
                    ins.then_inc(chain, 1)
                    dve.wait_ge(chain, count[0])

                dve.wait_ge(chosen, B1)
                member3 = member2[:, :].rearrange("p (e t) -> p e t", e=E2)
                wide = [P, E2, B1]
                link(dve.tensor_tensor(member3, iota[:, 0:E2, None].to_broadcast(wide),
                                       choice[:, None, :].to_broadcast(wide), ALU.is_equal))
                link(dve.tensor_tensor(member3, member3, valid1[:, None, :].to_broadcast(wide), ALU.mult))
                means = w_mean[:, :].rearrange("p (e k) -> p k e", k=3)

                def last_steps():
                    step_inverse(dve, At(B1 - 1))
                    m = At(MATS - LATE - 1)
                    mean_of(dve, m)
                    scale_of(dve, m)
                    scale_part(dve, m)

                def late_scale(i):
                    one = slice(MATS - LATE + i, MATS - LATE + i + 1)
                    dve.wait_ge(mean_ready, MATS - LATE + i + 1)
                    dve.tensor_scalar(w_mean[:, one], bank[5][:, i:i + 1], 1.0 / (D * D), EPS, ALU.mult, ALU.max)\
                        .then_inc(late, 1)
                    dve.wait_ge(late, 2 * i + 1)
                    dve.reciprocal(w_scale[:, one], w_mean[:, one]).then_inc(late, 1)

                def first_late_scale():
                    late_scale(0)

                sort_vector(dve, link, member2, E2, B1, B2, table1, expert2, gather2, store2, hots2, 1,
                            last_steps, first_late_scale)
                late_scale(1)
                link(dve.tensor_tensor(gu_mean[:, :], means[:, 0, :], means[:, 0, :], ALU.mult))
                dve.wait_ge(late, 4)
                dve.tensor_scalar(d_mean[:, :], means[:, 2, :], 1.0 / (QMAX * QMAX), None, ALU.mult)
                link(dve.scalar_tensor_tensor(gu_mean[:, :], gu_mean[:, :], QMAX, means[:, 1, :],
                                              ALU.mult, ALU.mult))
                cut(dve, At(MATS - LATE - 1), At(4 * (MATS - LATE) - 1))

                def late_cut(i):
                    m = MATS - LATE + i
                    dve.wait_ge(tern_act, m + 1)
                    cols = slice(m * K * D, (m + 1) * K * D)
                    dve.tensor_scalar(ternary[:, cols], ternary[:, cols].bitcast(I16), 1.0, -1.0,
                                      ALU.min, ALU.max).then_inc(late, 1)

                late_cut(0)
                wide = [P, B2, E2]
                is_expert = scan[:, 0:B2 * E2].rearrange("p (b e) -> p b e", b=B2)
                picked = placed[:, 0:B2 * E2].rearrange("p (b e) -> p b e", b=B2)
                link(dve.tensor_tensor(is_expert, iota[:, None, 0:E2].to_broadcast(wide),
                                       expert_f[:, 0:B2, None].to_broadcast(wide), ALU.is_equal))
                for mean, by_block in ((gu_mean, gu_block), (d_mean, d_block)):
                    link(dve.tensor_tensor(picked, is_expert, mean[:, None, :].to_broadcast(wide), ALU.mult))
                    link(dve.tensor_reduce(by_block[:, :], picked, X, ALU.add))
                late_cut(1)

                def tick(t):
                    b = t - 1
                    if b.within(0, B2):
                        dve.wait_ge(prod_ready, (b + 1).v)
                        dve.tensor_reduce(fac[b % 2][:, 0:1], prod[b % 2][:, :], X, ALU.max,
                                          apply_absolute_value=True).then_inc(amax_ready, 1)
                    b = t - 4
                    if b.within(0, B2):
                        dve.wait_ge(d_ready, (b + 1).v)
                        dve.wait_ge(factors, (b * 4 + 4).v)
                        dve.scalar_tensor_tensor(row_of(b, 0, D), d_ps[:, :], out_scale[:, bass.ds(b.v, 1)], row_of(b, 0, D),
                                                 ALU.mult, ALU.add).then_inc(out_ready, 1)
                    b = t - 1
                    if b.within(0, B2):
                        f = fac[b % 2]
                        dve.wait_ge(amax_ready, (b + 1).v)
                        dve.wait_ge(size_ready, (b + 1).v)
                        dve.tensor_scalar(f[:, 2:3], f[:, 0:1], f[:, 1:2], QMAX * EPS, ALU.mult, ALU.max)\
                            .then_inc(factors, 1)
                    b = t
                    if b.within(0, B2):
                        dve.tensor_scalar(fac[b % 2][:, 1:2], row_of(b, CUBE_COL, 1), gu_block[:, bass.ds(b.v, 1)], None,
                                          ALU.mult).then_inc(size_ready, 1)
                    b = t - 1
                    if b.within(0, B2):
                        f = fac[b % 2]
                        dve.wait_ge(factors, (b * 4 + 1).v)
                        dve.reciprocal(f[:, 4:5], f[:, 2:3]).then_inc(factors, 1)
                        dve.tensor_scalar(out_scale[:, bass.ds(b.v, 1)], f[:, 2:3], d_block[:, bass.ds(b.v, 1)], None,
                                          ALU.mult).then_inc(factors, 1)
                        dve.wait_ge(factors, (b * 4 + 2).v)
                        dve.tensor_scalar(f[:, 3:4], f[:, 1:2], f[:, 4:5], QMAX, ALU.mult, ALU.mult)\
                            .then_inc(factors, 1)
                    b = t + 1
                    if b.within(0, B2):
                        dve.wait_ge(tT_ready, (b + 1).v)
                        if b >= 2:
                            dve.wait_ge(u_ready, (b - 1).v)
                        dve.tensor_copy(qT[b % 2][:, :], tT_ps[b % 2].bitcast(I16)).then_inc(qT_ready, 1)
                    b = t
                    if b.within(0, B2):
                        dve.wait_ge(u_ready, (b + 1).v)
                        dve.wait_ge(relu2_ready, (b + 1).v)
                        if b >= 2:
                            dve.wait_ge(r8_ready, (b - 1).v)
                        dve.tensor_tensor(prod[b % 2][:, :], u_ps[b % 2][:, :], relu2[:, :], ALU.mult)\
                            .then_inc(prod_ready, 1)

                run_ticks(dve, T2_FIRST, T2_LAST, T2_LOOP, T2_UNROLL, T2_TURNS, tick)

            @block.tensor
            def _(pe):
                def late_mean(i):
                    m = MATS - LATE + i
                    pe.wait_ge(abs_ready, m + 1)
                    if i >= 1:
                        pe.wait_ge(late, 2 * i)
                    pe.matmul(bank[5][:, i:i + 1], ones[:, 0:P], abs_sum[:, m:m + 1], start=True,
                              stop=True).then_inc(mean_ready, 1)

                def first_late_mean():
                    late_mean(0)

                sort_tensor(pe, member2, E2, B1, B2, hots2, TILES, 1,
                            first_late_mean)
                late_mean(1)

                def transpose(ps, src):
                    for k in range(K):
                        last = pe.transpose(ps[:, k * P:(k + 1) * P], src[:, k * P:(k + 1) * P].bitcast(BF16),
                                            ident16[:, :])
                    return last

                def product(ps, left, e, kind):
                    for k in range(K):
                        last = pe.matmul(ps[:, :], left[:, k * P:(k + 1) * P],
                                         ternary[:, bass.ds(e * (3 * K * D) + (kind * K + k) * D, D)],
                                         start=(k == 0), stop=(k == K - 1))
                    return last

                def expert_of(b):
                    return pe.value_load(expert2[0:1, bass.ds(b.v, 1)], min_val=0, max_val=E2 - 1)

                def tick(t):
                    b = t + 1
                    if b.within(0, B2):
                        pe.wait_ge(t8_ready, (b + 1).v)
                        if b >= 2:
                            pe.wait_ge(qT_ready, (b - 1).v)
                        transpose(tT_ps[b % 2], t8[b % 2]).then_inc(tT_ready, 1)
                    e = expert_of(t) if t.within(0, B2) else None
                    b = t
                    if b.within(0, B2):
                        pe.wait_ge(qT_ready, (b + 1).v)
                        if b >= 2:
                            pe.wait_ge(prod_ready, (b - 1).v)
                        if b.turn is None and b.first == 0:
                            pe.wait_ge(tern, 4 * (MATS - LATE))
                            pe.wait_ge(late, 3 * LATE)
                        product(g_ps[b % 2], qT[b % 2], e, 0).then_inc(g_ready, 1)
                        product(u_ps[b % 2], qT[b % 2], e, 1).then_inc(u_ready, 1)
                    e_down = expert_of(t - 3) if (t - 3).within(0, B2) else None
                    b = t - 2
                    if b.within(0, B2):
                        pe.wait_ge(r8_ready, (b + 1).v)
                        if b >= 1:
                            pe.wait_ge(rT_ready, b.v)
                        transpose(rT_ps, r8).then_inc(rT_ps_ready, 1)
                    b = t - 3
                    if b.within(0, B2):
                        pe.wait_ge(rT_ready, (b + 1).v)
                        if b >= 1:
                            pe.wait_ge(out_ready, b.v)
                        product(d_ps, rT[b % 2], e_down, 2).then_inc(d_ready, 1)

                pe.wait_ge(experts_ready, 2)
                warm_up(pe, WARM_UP2)
                run_ticks(pe, T2_FIRST, T2_LAST, T2_LOOP, T2_UNROLL, T2_TURNS, tick)

            stack.pop()


def kernel(x, itok_BxS_13_99985, ctx_2048, L0_ffn_router_w, L0_ffn_wg, L0_ffn_wu, L0_ffn_wd):
    import numpy as np
    import concourse.bacc as bacc
    from concourse.bass_utils import run_bass_kernel_spmd

    def chunked(w):
        n = w.shape[0]
        w = w.transpose(0, 2, 1).reshape(n, K, P, w.shape[1])
        return np.ascontiguousarray(w.transpose(0, 2, 1, 3).reshape(n, P, -1))

    wg, wu, wd = (np.asarray(w) for w in (L0_ffn_wg, L0_ffn_wu, L0_ffn_wd))
    arrays = {
        "x_rows": np.ascontiguousarray(np.asarray(x).reshape(N, D)),
        "token_ids_in": np.ascontiguousarray(np.asarray(itok_BxS_13_99985).reshape(TILES, P).T),
        "ctx_chunks": chunked(np.asarray(ctx_2048)),
        "router_chunks": chunked(np.asarray(L0_ffn_router_w)[None])[0],
        "weight_chunks": chunked(np.stack([wg, wu, wd], axis=1).reshape(MATS, D, D)),
    }
    nc = bacc.Bacc("TRN2", target_bir_lowering=False, num_devices=1, dynamic_dma_scratch_size=4096)
    args = [nc.dram_tensor(name, a.shape, mybir.dt.from_np(a.dtype), kind="ExternalInput").ap()
            for name, a in arrays.items()]
    out = nc.dram_tensor("out_rows", (N, D), F32, kind="ExternalOutput").ap()
    moe_program(nc, *args, out)
    r = run_bass_kernel_spmd(nc, [arrays], core_ids=[0])
    return np.asarray(r.results[0]["out_rows"]).reshape(np.asarray(x).shape)
```
